# Optimizing a Trainium2 kernel written in Bass

```python
import numpy as np
import jax
import jax.numpy as jnp

def _softmax(x, axis=-1):
    return jax.nn.softmax(x, axis=axis)

def _gelu(x):
    return jax.nn.gelu(x, approximate=True)

def _silu(x):
    return jax.nn.silu(x)

def _sigmoid(x):
    return jax.nn.sigmoid(x)

def _layernorm(x, axis=-1, eps=1e-05):
    m = jnp.mean(x, axis=axis, keepdims=True)
    v = jnp.var(x, axis=axis, keepdims=True)
    return (x - m) / jnp.sqrt(v + eps)

def _scatter_add(tgt, idx, src, axis=0):
    return tgt.at[idx].add(src)

def _segment_sum(src, seg, n):
    return jax.ops.segment_sum(src, seg, n)
kernel_name = 'mk_lm_tower_d2_tok_ids256_r4_293bbf'

def setup_inputs(seed: int=0):
    np.random.seed(seed)
    _w = jnp.asarray

    def _rec_inputs():
        import jax
        import jax.numpy as jnp
        _rk = jax.random.key(seed)
        x = jax.random.randint(jax.random.fold_in(_rk, 1), (128, 128), 0, 100001, jnp.int32)
        return x
    x = _rec_inputs()

    def _L0_tok_setup():
        import jax, jax.numpy as jnp
        import numpy as np
        NUM_ITEMS = 25000
        D = 64
        FOURIER_DIM = 64
        VISIT_DIM = 24
        RESIDUAL_SCALE = 0.1
        LN_EPS = 1e-05

        def _layer_norm(x, gamma, beta):
            mu = jnp.mean(x, axis=-1, keepdims=True)
            var = jnp.mean(jnp.square(x - mu), axis=-1, keepdims=True)
            return (x - mu) * jax.lax.rsqrt(var + LN_EPS) * gamma + beta
        key = jax.random.key(seed)
        ks = jax.random.split(key, 12)
        item_ids = jax.random.randint(ks[0], (128, 512), 0, NUM_ITEMS + 1)
        emb_table = 0.02 * jax.random.normal(ks[1], (NUM_ITEMS + 1, D), dtype=jnp.float32)
        emb_table = emb_table.at[0].set(0.0)
        geo_table = jax.random.normal(ks[2], (NUM_ITEMS + 1, FOURIER_DIM), dtype=jnp.float32)
        visit_table = jax.random.uniform(ks[3], (NUM_ITEMS + 1, VISIT_DIM), dtype=jnp.float32)

        def xavier(k, fan_in, fan_out):
            lim = np.sqrt(6.0 / (fan_in + fan_out))
            return jax.random.uniform(k, (fan_in, fan_out), jnp.float32, -lim, lim)
        w_item = xavier(ks[4], D, D)
        b_item = jnp.zeros((D,), jnp.float32)
        w_geo = xavier(ks[5], FOURIER_DIM, D)
        b_geo = jnp.zeros((D,), jnp.float32)
        w_visit = xavier(ks[6], VISIT_DIM, D)
        b_visit = jnp.zeros((D,), jnp.float32)
        w_fuse = xavier(ks[7], 3 * D, D)
        b_fuse = jnp.zeros((D,), jnp.float32)
        ln_gamma = jnp.ones((D,), jnp.float32)
        ln_beta = jnp.zeros((D,), jnp.float32)
        return dict(item_ids=item_ids, emb_table=emb_table, geo_table=geo_table, visit_table=visit_table, w_item=w_item, b_item=b_item, w_geo=w_geo, b_geo=b_geo, w_visit=w_visit, b_visit=b_visit, w_fuse=w_fuse, b_fuse=b_fuse, ln_gamma=ln_gamma, ln_beta=ln_beta)
    _L0_tok_all = _L0_tok_setup()
    _L0_tok_in = {k: v for k, v in _L0_tok_all.items() if k in ('emb_table', 'geo_table', 'visit_table', 'w_item', 'b_item', 'w_geo', 'b_geo', 'w_visit', 'b_visit', 'w_fuse', 'b_fuse', 'ln_gamma', 'ln_beta')}
    del _L0_tok_all

    def _L0_attn_setup():
        import jax, jax.numpy as jnp
        import numpy as np
        B_, L_, D_ = (8, 512, 64)
        DIN, N_, P_ = (128, 64, 64)
        H_ = DIN // P_

        def _ln(x, w, b, eps=1e-05):
            m = x.mean(-1, keepdims=True)
            v = ((x - m) ** 2).mean(-1, keepdims=True)
            return (x - m) * jax.lax.rsqrt(v + eps) * w + b
        key = jax.random.key(seed)
        ks = jax.random.split(key, 8)
        s = lambda k, shape, sc: jax.random.normal(k, shape, jnp.float32) * sc
        return dict(src=jax.random.normal(ks[0], (B_, L_, D_), jnp.float32), ln_w=jnp.ones((D_,), jnp.float32), ln_b=jnp.zeros((D_,), jnp.float32), W_in=s(ks[1], (D_, DIN), 0.02), conv_w=s(ks[2], (DIN, 1, 3), 0.1), conv_b=jnp.zeros((DIN,), jnp.float32), W_xproj=s(ks[3], (DIN, H_ + 2 * N_), 0.02), dt_bias=s(ks[4], (H_,), 0.1), A_log=jnp.log(jnp.arange(1, H_ + 1, dtype=jnp.float32)), Ds=jnp.ones((H_,), jnp.float32), oln_w=jnp.ones((DIN,), jnp.float32), oln_b=jnp.zeros((DIN,), jnp.float32), W_out=s(ks[5], (DIN, D_), 0.02))
    _L0_attn_all = _L0_attn_setup()
    _L0_attn_in = {k: v for k, v in _L0_attn_all.items() if k in ('ln_w', 'ln_b', 'W_in', 'conv_w', 'conv_b', 'W_xproj', 'dt_bias', 'A_log', 'Ds', 'oln_w', 'oln_b', 'W_out')}
    del _L0_attn_all

    def _L0_ffn_setup():
        import jax, jax.numpy as jnp
        import numpy as np
        DIM = 64
        HEADS = 8
        NUM_KEYS = 64
        NUM_KV = NUM_KEYS ** 2
        PK_TOPK = 16
        FINAL_TOPK = 16
        DIM_KEY = DIM // 2
        P = 2

        def _pk(x, Wq_pk, pk_keys):
            b, n, _ = x.shape
            q = (x @ Wq_pk).reshape(b, n, P, HEADS, DIM_KEY).transpose(2, 0, 1, 3, 4)
            sim = jnp.einsum('pbnhd,pkhd->pbnhk', q, pk_keys)
            scores, idx = jax.lax.top_k(sim, PK_TOPK)
            idx0 = idx[0]
            idx1 = idx[1] * NUM_KEYS
            index = (idx0[..., :, None] + idx1[..., None, :]).reshape(b, n, HEADS, PK_TOPK * PK_TOPK)
            score = (scores[0][..., :, None] + scores[1][..., None, :]).reshape(b, n, HEADS, PK_TOPK * PK_TOPK)
            final_scores, pk_idx = jax.lax.top_k(score, FINAL_TOPK)
            final_indices = jnp.take_along_axis(index, pk_idx, axis=-1)
            final_scores = jax.nn.softmax(final_scores, axis=-1)
            return (final_scores, final_indices)
        key = jax.random.key(seed)
        ks = jax.random.split(key, 7)
        b, n = (2, 256)
        std = 0.02
        x = jax.random.normal(ks[0], (b, n, DIM), dtype=jnp.float32)
        Wq_pk = jax.random.normal(ks[1], (DIM, P * HEADS * DIM_KEY), dtype=jnp.float32) * std
        pk_keys = jax.random.normal(ks[2], (P, NUM_KEYS, HEADS, DIM_KEY), dtype=jnp.float32) * std
        Wq = jax.random.normal(ks[3], (DIM, HEADS * DIM), dtype=jnp.float32) * std
        keys_table = jax.random.normal(ks[4], (NUM_KV * HEADS, DIM), dtype=jnp.float32) * std
        values_table = jax.random.normal(ks[5], (NUM_KV * HEADS, DIM), dtype=jnp.float32) * std
        Wo = jax.random.normal(ks[6], (DIM * HEADS, DIM), dtype=jnp.float32) * std
        return {'x': x, 'Wq_pk': Wq_pk, 'pk_keys': pk_keys, 'Wq': Wq, 'keys_table': keys_table, 'values_table': values_table, 'Wo': Wo}
    _L0_ffn_all = _L0_ffn_setup()
    _L0_ffn_in = {k: v for k, v in _L0_ffn_all.items() if k in ('Wq_pk', 'pk_keys', 'Wq', 'keys_table', 'values_table', 'Wo')}
    del _L0_ffn_all

    def _L1_attn_setup():
        import jax, jax.numpy as jnp
        import numpy as np
        import math
        B, S, D = (4, 1024, 64)
        key = jax.random.key(seed)
        ks = jax.random.split(key, 9)
        s = 1.0 / math.sqrt(D)
        return {'src': jax.random.normal(ks[0], (B, S, D), dtype=jnp.float32), 'Wq': jax.random.normal(ks[1], (D, D), dtype=jnp.float32) * s, 'bq': jax.random.normal(ks[2], (D,), dtype=jnp.float32) * s, 'Wk': jax.random.normal(ks[3], (D, D), dtype=jnp.float32) * s, 'bk': jax.random.normal(ks[4], (D,), dtype=jnp.float32) * s, 'Wv': jax.random.normal(ks[5], (D, D), dtype=jnp.float32) * s, 'bv': jax.random.normal(ks[6], (D,), dtype=jnp.float32) * s, 'Wo': jax.random.normal(ks[7], (D, D), dtype=jnp.float32) * s, 'bo': jax.random.normal(ks[8], (D,), dtype=jnp.float32) * s}
    _L1_attn_all = _L1_attn_setup()
    _L1_attn_in = {k: v for k, v in _L1_attn_all.items() if k in ('Wq', 'bq', 'Wk', 'bk', 'Wv', 'bv', 'Wo', 'bo')}
    del _L1_attn_all

    def _L1_ffn_setup():
        import jax, jax.numpy as jnp
        import numpy as np
        E, D, H, TOP_K = (6, 64, 64, 2)
        ROUTER_H = D // 2
        key = jax.random.key(seed)
        ks = jax.random.split(key, 12)
        s = 1.0 / np.sqrt(D)
        sh = 1.0 / np.sqrt(H)
        sr = 1.0 / np.sqrt(ROUTER_H)
        return {'features': jax.random.normal(ks[0], (8, 1024, D), dtype=jnp.float32), 'router_w1': jax.random.uniform(ks[1], (D, ROUTER_H), jnp.float32, -s, s), 'router_b1': jnp.zeros((ROUTER_H,), jnp.float32), 'router_w2': jax.random.uniform(ks[2], (ROUTER_H, E), jnp.float32, -sr, sr), 'router_b2': jnp.zeros((E,), jnp.float32), 'expert_w1': jax.random.uniform(ks[3], (E, D, H), jnp.float32, -s, s), 'expert_b1': jnp.zeros((E, H), jnp.float32), 'expert_w2': jax.random.uniform(ks[4], (E, H, H), jnp.float32, -sh, sh), 'expert_b2': jnp.zeros((E, H), jnp.float32), 'expert_w3': jax.random.uniform(ks[5], (E, H, D), jnp.float32, -sh, sh), 'expert_b3': jnp.zeros((E, D), jnp.float32)}
    _L1_ffn_all = _L1_ffn_setup()
    _L1_ffn_in = {k: v for k, v in _L1_ffn_all.items() if k in ('router_w1', 'router_b1', 'router_w2', 'router_b2', 'expert_w1', 'expert_b1', 'expert_w2', 'expert_b2', 'expert_w3', 'expert_b3')}
    del _L1_ffn_all
    return {'x': x, 'L0_tok_emb_table': _L0_tok_in['emb_table'], 'L0_tok_geo_table': _L0_tok_in['geo_table'], 'L0_tok_visit_table': _L0_tok_in['visit_table'], 'L0_tok_w_item': _L0_tok_in['w_item'], 'L0_tok_b_item': _L0_tok_in['b_item'], 'L0_tok_w_geo': _L0_tok_in['w_geo'], 'L0_tok_b_geo': _L0_tok_in['b_geo'], 'L0_tok_w_visit': _L0_tok_in['w_visit'], 'L0_tok_b_visit': _L0_tok_in['b_visit'], 'L0_tok_w_fuse': _L0_tok_in['w_fuse'], 'L0_tok_b_fuse': _L0_tok_in['b_fuse'], 'L0_tok_ln_gamma': _L0_tok_in['ln_gamma'], 'L0_tok_ln_beta': _L0_tok_in['ln_beta'], 'L0_attn_ln_w': _L0_attn_in['ln_w'], 'L0_attn_ln_b': _L0_attn_in['ln_b'], 'L0_attn_W_in': _L0_attn_in['W_in'], 'L0_attn_conv_w': _L0_attn_in['conv_w'], 'L0_attn_conv_b': _L0_attn_in['conv_b'], 'L0_attn_W_xproj': _L0_attn_in['W_xproj'], 'L0_attn_dt_bias': _L0_attn_in['dt_bias'], 'L0_attn_A_log': _L0_attn_in['A_log'], 'L0_attn_Ds': _L0_attn_in['Ds'], 'L0_attn_oln_w': _L0_attn_in['oln_w'], 'L0_attn_oln_b': _L0_attn_in['oln_b'], 'L0_attn_W_out': _L0_attn_in['W_out'], 'L0_ffn_Wq_pk': _L0_ffn_in['Wq_pk'], 'L0_ffn_pk_keys': _L0_ffn_in['pk_keys'], 'L0_ffn_Wq': _L0_ffn_in['Wq'], 'L0_ffn_keys_table': _L0_ffn_in['keys_table'], 'L0_ffn_values_table': _L0_ffn_in['values_table'], 'L0_ffn_Wo': _L0_ffn_in['Wo'], 'L1_attn_Wq': _L1_attn_in['Wq'], 'L1_attn_bq': _L1_attn_in['bq'], 'L1_attn_Wk': _L1_attn_in['Wk'], 'L1_attn_bk': _L1_attn_in['bk'], 'L1_attn_Wv': _L1_attn_in['Wv'], 'L1_attn_bv': _L1_attn_in['bv'], 'L1_attn_Wo': _L1_attn_in['Wo'], 'L1_attn_bo': _L1_attn_in['bo'], 'L1_ffn_router_w1': _L1_ffn_in['router_w1'], 'L1_ffn_router_b1': _L1_ffn_in['router_b1'], 'L1_ffn_router_w2': _L1_ffn_in['router_w2'], 'L1_ffn_router_b2': _L1_ffn_in['router_b2'], 'L1_ffn_expert_w1': _L1_ffn_in['expert_w1'], 'L1_ffn_expert_b1': _L1_ffn_in['expert_b1'], 'L1_ffn_expert_w2': _L1_ffn_in['expert_w2'], 'L1_ffn_expert_b2': _L1_ffn_in['expert_b2'], 'L1_ffn_expert_w3': _L1_ffn_in['expert_w3'], 'L1_ffn_expert_b3': _L1_ffn_in['expert_b3']}

def reference(x, L0_tok_emb_table, L0_tok_geo_table, L0_tok_visit_table, L0_tok_w_item, L0_tok_b_item, L0_tok_w_geo, L0_tok_b_geo, L0_tok_w_visit, L0_tok_b_visit, L0_tok_w_fuse, L0_tok_b_fuse, L0_tok_ln_gamma, L0_tok_ln_beta, L0_attn_ln_w, L0_attn_ln_b, L0_attn_W_in, L0_attn_conv_w, L0_attn_conv_b, L0_attn_W_xproj, L0_attn_dt_bias, L0_attn_A_log, L0_attn_Ds, L0_attn_oln_w, L0_attn_oln_b, L0_attn_W_out, L0_ffn_Wq_pk, L0_ffn_pk_keys, L0_ffn_Wq, L0_ffn_keys_table, L0_ffn_values_table, L0_ffn_Wo, L1_attn_Wq, L1_attn_bq, L1_attn_Wk, L1_attn_bk, L1_attn_Wv, L1_attn_bv, L1_attn_Wo, L1_attn_bo, L1_ffn_router_w1, L1_ffn_router_b1, L1_ffn_router_w2, L1_ffn_router_b2, L1_ffn_expert_w1, L1_ffn_expert_b1, L1_ffn_expert_w2, L1_ffn_expert_b2, L1_ffn_expert_w3, L1_ffn_expert_b3):
    import jax
    import jax.numpy as jnp

    def _L0_tok_ref(item_ids, emb_table, geo_table, visit_table, w_item, b_item, w_geo, b_geo, w_visit, b_visit, w_fuse, b_fuse, ln_gamma, ln_beta):
        import jax, jax.numpy as jnp
        import numpy as np
        NUM_ITEMS = 25000
        D = 64
        FOURIER_DIM = 64
        VISIT_DIM = 24
        RESIDUAL_SCALE = 0.1
        LN_EPS = 1e-05

        def _layer_norm(x, gamma, beta):
            mu = jnp.mean(x, axis=-1, keepdims=True)
            var = jnp.mean(jnp.square(x - mu), axis=-1, keepdims=True)
            return (x - mu) * jax.lax.rsqrt(var + LN_EPS) * gamma + beta
        gelu = lambda x: jax.nn.gelu(x, approximate=False)
        safe_ids = jnp.clip(item_ids, 0, emb_table.shape[0] - 1)
        item_emb = emb_table[safe_ids]
        fourier_feat = geo_table[safe_ids]
        visit_feat = visit_table[safe_ids]
        item_h = gelu(item_emb @ w_item + b_item)
        geo_h = gelu(fourier_feat @ w_geo + b_geo)
        visit_h = gelu(visit_feat @ w_visit + b_visit)
        cat = jnp.concatenate([item_h, geo_h, visit_h], axis=-1)
        fused = _layer_norm(gelu(cat @ w_fuse + b_fuse), ln_gamma, ln_beta)
        valid_mask = (item_ids != 0)[..., None].astype(fused.dtype)
        fused = fused * valid_mask
        return item_emb + RESIDUAL_SCALE * fused

    def _L0_attn_ref(src, ln_w, ln_b, W_in, conv_w, conv_b, W_xproj, dt_bias, A_log, Ds, oln_w, oln_b, W_out):
        import jax, jax.numpy as jnp
        import numpy as np
        B_, L_, D_ = (8, 512, 64)
        DIN, N_, P_ = (128, 64, 64)
        H_ = DIN // P_

        def _ln(x, w, b, eps=1e-05):
            m = x.mean(-1, keepdims=True)
            v = ((x - m) ** 2).mean(-1, keepdims=True)
            return (x - m) * jax.lax.rsqrt(v + eps) * w + b
        B, L, D = src.shape
        H, N, P = (H_, N_, P_)
        x = _ln(src, ln_w, ln_b)
        u = x @ W_in
        uc = jax.lax.conv_general_dilated(u.transpose(0, 2, 1), conv_w, (1,), 'SAME', feature_group_count=DIN, dimension_numbers=('NCH', 'OIH', 'NCH'))
        u = jax.nn.gelu((uc + conv_b[None, :, None]).transpose(0, 2, 1), approximate=False)
        dbc = u @ W_xproj
        dt = jax.nn.softplus(dbc[..., :H] + dt_bias)
        Bm = dbc[..., H:H + N]
        Cm = dbc[..., H + N:]
        A = -jnp.exp(A_log)
        decay = jnp.exp(dt * A)
        xh = u.reshape(B, L, H, P)
        dtx = dt[..., None] * xh

        def step(h, inp):
            dec_t, dtx_t, B_t, C_t = inp
            h = h * dec_t[:, :, None, None] + dtx_t[..., None] * B_t[:, None, None, :]
            y = jnp.einsum('bhpn,bn->bhp', h, C_t)
            return (h, y)
        h0 = jnp.zeros((B, H, P, N), u.dtype)
        inputs = (decay.transpose(1, 0, 2), dtx.transpose(1, 0, 2, 3), Bm.transpose(1, 0, 2), Cm.transpose(1, 0, 2))
        _, ys = jax.lax.scan(step, h0, inputs)
        y = ys.transpose(1, 0, 2, 3) + xh * Ds[None, None, :, None]
        y = _ln(y.reshape(B, L, DIN), oln_w, oln_b)
        return src + y @ W_out

    def _L0_ffn_ref(x, Wq_pk, pk_keys, Wq, keys_table, values_table, Wo):
        import jax, jax.numpy as jnp
        import numpy as np
        DIM = 64
        HEADS = 8
        NUM_KEYS = 64
        NUM_KV = NUM_KEYS ** 2
        PK_TOPK = 16
        FINAL_TOPK = 16
        DIM_KEY = DIM // 2
        P = 2

        def _pk(x, Wq_pk, pk_keys):
            b, n, _ = x.shape
            q = (x @ Wq_pk).reshape(b, n, P, HEADS, DIM_KEY).transpose(2, 0, 1, 3, 4)
            sim = jnp.einsum('pbnhd,pkhd->pbnhk', q, pk_keys)
            scores, idx = jax.lax.top_k(sim, PK_TOPK)
            idx0 = idx[0]
            idx1 = idx[1] * NUM_KEYS
            index = (idx0[..., :, None] + idx1[..., None, :]).reshape(b, n, HEADS, PK_TOPK * PK_TOPK)
            score = (scores[0][..., :, None] + scores[1][..., None, :]).reshape(b, n, HEADS, PK_TOPK * PK_TOPK)
            final_scores, pk_idx = jax.lax.top_k(score, FINAL_TOPK)
            final_indices = jnp.take_along_axis(index, pk_idx, axis=-1)
            final_scores = jax.nn.softmax(final_scores, axis=-1)
            return (final_scores, final_indices)
        b, n, d = x.shape
        q = (x @ Wq).reshape(b, n, HEADS, DIM) * DIM ** (-0.5)
        kv_scores, indices = _pk(x, Wq_pk, pk_keys)
        offsets = jnp.arange(HEADS, dtype=indices.dtype) * NUM_KV
        ind = indices + offsets[None, None, :, None]
        k = jnp.einsum('bnhk,bnhkd->bnhd', kv_scores, keys_table[ind])
        v = jnp.einsum('bnhk,bnhkd->bnhd', kv_scores, values_table[ind])
        sim = jnp.einsum('bihd,bjhd->bhij', q, k)
        neg = -jnp.finfo(sim.dtype).max
        causal = jnp.tril(jnp.ones((n, n), dtype=bool))
        sim = jnp.where(causal, sim, neg)
        attn = jax.nn.softmax(sim, axis=-1)
        out = jnp.einsum('bhij,bjhd->bhid', attn, v)
        out = out.transpose(0, 2, 1, 3).reshape(b, n, HEADS * DIM)
        return out @ Wo

    def _L1_attn_ref(src, Wq, bq, Wk, bk, Wv, bv, Wo, bo):
        import jax, jax.numpy as jnp
        import numpy as np
        import math
        B, S, D = (4, 1024, 64)
        q = src @ Wq.T + bq
        k = src @ Wk.T + bk
        v = src @ Wv.T + bv
        row_mask = (q[:, :, 0] != 0) & (k[:, :, 0] != 0)
        mask = row_mask[:, :, None]
        scale = 1.0 / math.sqrt(D)
        scores = jnp.einsum('bid,bjd->bij', q, k) * scale
        scores = jnp.where(mask, scores, jnp.float32(-1000000000.0))
        prob = jax.nn.softmax(scores, axis=-1)
        prob = jnp.where(mask, prob, 0.0)
        out = jnp.einsum('bij,bjd->bid', prob, v)
        return out @ Wo.T + bo

    def _L1_ffn_ref(features, router_w1, router_b1, router_w2, router_b2, expert_w1, expert_b1, expert_w2, expert_b2, expert_w3, expert_b3):
        import jax, jax.numpy as jnp
        import numpy as np
        E, D, H, TOP_K = (6, 64, 64, 2)
        ROUTER_H = D // 2
        rh = jax.nn.relu(features @ router_w1 + router_b1)
        expert_logits = jax.nn.softmax(rh @ router_w2 + router_b2, axis=-1)
        top_w, top_i = jax.lax.top_k(expert_logits, TOP_K)
        routing_weights = jax.nn.softmax(top_w, axis=-1)
        h1 = jax.nn.relu(jnp.einsum('bsd,edh->bseh', features, expert_w1) + expert_b1)
        h2 = jax.nn.relu(jnp.einsum('bseh,ehf->bsef', h1, expert_w2) + expert_b2)
        expert_out = jnp.einsum('bsef,efo->bseo', h2, expert_w3) + expert_b3
        sel = jnp.take_along_axis(expert_out, top_i[:, :, :, None], axis=2)
        combined = jnp.sum(sel * routing_weights[..., None], axis=2)
        return combined
    h = _L0_tok_ref(x, L0_tok_emb_table, L0_tok_geo_table, L0_tok_visit_table, L0_tok_w_item, L0_tok_b_item, L0_tok_w_geo, L0_tok_b_geo, L0_tok_w_visit, L0_tok_b_visit, L0_tok_w_fuse, L0_tok_b_fuse, L0_tok_ln_gamma, L0_tok_ln_beta)
    h = h + _L0_attn_ref(_layernorm(h, axis=-1), L0_attn_ln_w, L0_attn_ln_b, L0_attn_W_in, L0_attn_conv_w, L0_attn_conv_b, L0_attn_W_xproj, L0_attn_dt_bias, L0_attn_A_log, L0_attn_Ds, L0_attn_oln_w, L0_attn_oln_b, L0_attn_W_out)
    h = h + _L0_ffn_ref(_layernorm(h, axis=-1), L0_ffn_Wq_pk, L0_ffn_pk_keys, L0_ffn_Wq, L0_ffn_keys_table, L0_ffn_values_table, L0_ffn_Wo)
    h = h + _L1_attn_ref(_layernorm(h, axis=-1), L1_attn_Wq, L1_attn_bq, L1_attn_Wk, L1_attn_bk, L1_attn_Wv, L1_attn_bv, L1_attn_Wo, L1_attn_bo)
    h = h + _L1_ffn_ref(_layernorm(h, axis=-1), L1_ffn_router_w1, L1_ffn_router_b1, L1_ffn_router_w2, L1_ffn_router_b2, L1_ffn_expert_w1, L1_ffn_expert_b1, L1_ffn_expert_w2, L1_ffn_expert_b2, L1_ffn_expert_w3, L1_ffn_expert_b3)
    return h

_drawn_inputs = setup_inputs


def setup_inputs(seed=0):
    import zlib

    import numpy as np

    out = dict(_drawn_inputs(seed))
    spreads = {'L0_tok_b_item': (0.0, 0.1),
     'L0_tok_b_geo': (0.0, 0.1),
     'L0_tok_b_visit': (0.0, 0.1),
     'L0_tok_b_fuse': (0.0, 0.1),
     'L0_tok_ln_gamma': (1.0, 0.2),
     'L0_tok_ln_beta': (0.0, 0.1),
     'L0_attn_ln_w': (1.0, 0.6),
     'L0_attn_ln_b': (0.0, 0.512),
     'L0_attn_conv_b': (0.0, 0.1),
     'L0_attn_Ds': (1.0, 0.2),
     'L0_attn_oln_w': (1.0, 0.2),
     'L0_attn_oln_b': (0.0, 0.271),
     'L1_ffn_router_b1': (0.0, 0.1),
     'L1_ffn_router_b2': (0.0, 0.1),
     'L1_ffn_expert_b1': (0.0, 0.8),
     'L1_ffn_expert_b2': (0.0, 0.339),
     'L1_ffn_expert_b3': (0.0, 0.1)}
    factors = {'L0_attn_W_xproj': 59.01,
     'L0_attn_dt_bias': 23.306,
     'L0_attn_A_log': 22.799,
     'L0_ffn_Wq_pk': 8.0,
     'L0_ffn_pk_keys': 8.0,
     'L0_ffn_Wq': 64.0,
     'L0_ffn_keys_table': 64.0,
     'L0_ffn_values_table': 8.0,
     'L0_ffn_Wo': 8.0,
     'L1_attn_bq': 3.218,
     'L1_attn_bk': 64.0}
    for name, (base, spread) in spreads.items():
        noise = np.random.default_rng([zlib.crc32(name.encode()), seed]).standard_normal(out[name].shape)
        drawn = base * np.exp(spread * noise) if base else spread * noise
        out[name] = jnp.asarray(drawn.astype(out[name].dtype))
    for name, factor in factors.items():
        out[name] = (out[name] * factor).astype(out[name].dtype)
    return out
```

```python
from contextlib import ExitStack

import numpy as np

import concourse.bass as bass
from concourse import mybir

ALU = mybir.AluOpType
ACT = mybir.ActivationFunctionType
AX = mybir.AxisListType
F32 = mybir.dt.float32
I32 = mybir.dt.int32
U32 = mybir.dt.uint32

T = 128
D = 64
ITEM, GEO, VISIT = 64, 64, 24
FEAT = ITEM + GEO + VISIT
CH = 128
SSM_HEADS, STATE = 2, 64
HEADS, KEYS, TOP = 8, 64, 16
GROUPS = 2 * HEADS
DKEY = D // 2
CAND = [TOP // (i + 1) for i in range(TOP)]
NCAND = sum(CAND)
CAND_BLOCKS = [(0, 1, 16), (1, 1, 8), (2, 1, 5), (3, 1, 4), (4, 1, 3), (5, 3, 2), (8, 8, 1)]
EXPERTS, ROUTER = 6, 32
PAIRS = EXPERTS // 2
EPS = 1e-5
LOWEST = -3.0e38
LOG1P_TERMS = 8


def param_layout():
    sizes = [
        ("ident", T, T), ("causal", T, T), ("iota_cand", NCAND, T), ("head_offset", HEADS * TOP, T),
        ("iota_expert", EXPERTS, T), ("ones_row", T, 1),
        ("w_ig", 128, 128), ("b_ig", 1, 128), ("w_visit", D, VISIT), ("b_visit", 1, D),
        ("w_fuse_ig", D, 128), ("w_fuse_v", D, D + 1), ("gamma", D, T), ("beta", D, T),
        ("ln_w", 1, D), ("ln_b", 1, D), ("w_in", CH, D), ("conv_w", 3 * CH, D), ("conv_b", 1, CH),
        ("w_xproj", SSM_HEADS + 2 * STATE, CH), ("dt_bias", SSM_HEADS, T), ("a_log", SSM_HEADS, T),
        ("d_skip", 1, CH), ("oln_w", 1, CH), ("oln_b", 1, CH), ("w_out", D, CH),
        ("wq_pk_t", GROUPS * D, DKEY), ("pk_keys_t", GROUPS * KEYS, DKEY),
        ("wq", HEADS * D, D), ("wo", HEADS // 2 * D, 2 * D),
        ("a_q", D, D + 1), ("a_k", D, D + 1), ("a_v", D + 2, D + 1), ("a_o", D, D + 1),
        ("r_w1", ROUTER, D + 1), ("r_w2", EXPERTS, ROUTER + 1),
        ("e_w1", EXPERTS * D, D + 1), ("e_w2", PAIRS * 128, 128), ("e_b2", PAIRS, 128),
        ("e_w3", PAIRS * 128, 128), ("e_b3", EXPERTS * D, 1),
    ]
    at, out = 0, {}
    for name, cols, rows in sizes:
        out[name] = (at, cols, rows)
        at += cols
    return out, at


def build_program(nc, tokens, params, feature_table, memory_table, out):
    SEQS = tokens.shape[0]
    LAST_ITEM = feature_table.shape[0] - 1
    layout, _ = param_layout()
    ctx = ExitStack()
    with ctx:
        def sb(name, shape, dt=F32):
            return ctx.enter_context(nc.sbuf_tensor(name, shape, dt))

        def sem(name):
            return ctx.enter_context(nc.semaphore(name))

        P = sb("params_sb", [128, params.shape[1]])

        def par(name, rows=None):
            at, cols, r = layout[name]
            return P[0:rows or r, at:at + cols]

        w_tap = sb("w_tap", [D, 3, CH])
        neg_a = sb("neg_a", [T, SSM_HEADS])
        skip_diag = sb("skip_diag", [CH, CH])
        w_scores = sb("w_scores", [D, GROUPS * KEYS])
        eps_col = sb("eps_col", [T, 1])
        zero_col = sb("zero_col", [T, 1])
        tok_i = sb("tok_i", [SEQS, T], I32)
        tok_f = sb("tok_f", [SEQS, T])
        tok_ok = sb("tok_ok", [SEQS, T])
        tok_clip = sb("tok_clip", [SEQS, T])
        ids_t = sb("ids_t", [T, SEQS + 1], U32)
        ok_t = sb("ok_t", [T, SEQS])

        feat_idx = sb("feat_idx", [T, 1], U32)
        feat = [sb(f"feat{k}", [T, FEAT]) for k in range(2)]
        ig_t = sb("ig_t", [128, T])
        visit_t = sb("visit_t", [VISIT, T])
        igh_t = sb("igh_t", [128, T])
        vh_t = sb("vh_t", [D + 1, T])
        fused = sb("fused", [T, D])
        tok_mask = sb("tok_mask", [T, 1])
        stats = sb("stats", [T, 6])
        mv = sb("mv", [T, 2])
        std = sb("std", [T, 1])
        rstd = sb("rstd", [T, 1])
        tmp = [sb(f"tmp{k}", [T, D]) for k in range(2)]
        h0 = sb("h0", [T, D])
        src = sb("src", [T, D])
        xn = sb("xn", [T, D])
        x_t = sb("x_t", [D, T + 2])
        u_t = sb("u_t", [CH, T])
        bc_t = sb("bc_t", [STATE, 2 * T])
        z = sb("z", [T, SSM_HEADS])
        absz = sb("absz", [T, SSM_HEADS])
        ez = sb("ez", [T, SSM_HEADS])
        den = sb("den", [T, SSM_HEADS])
        s_at = sb("s_at", [T, SSM_HEADS])
        s_sq = sb("s_sq", [T, SSM_HEADS])
        poly = [sb(f"poly{k}", [T, SSM_HEADS]) for k in range(2)]
        dt_ = sb("dt", [T, SSM_HEADS])
        dt_a = sb("dt_a", [T, SSM_HEADS])
        decay = sb("decay", [T, SSM_HEADS])
        dtx = sb("dtx", [T, CH])
        l_t = sb("l_t", [T, SSM_HEADS, T])
        m_t = sb("m_t", [T, SSM_HEADS, T])
        yn = sb("yn", [T, CH])
        yn_t = sb("yn_t", [CH, T])
        h0s = sb("h0s", [T, D])
        h1 = [sb(f"h1_{k}", [T, D]) for k in range(2)]
        x2 = sb("x2", [T, D])
        x2_t = [sb(f"x2_t{k}", [D, T]) for k in range(2)]
        scores = sb("scores", [T, GROUPS, KEYS])
        scores2 = sb("scores2", [T, GROUPS, KEYS])
        top_s = sb("top_s", [T, GROUPS, TOP])
        top_i = sb("top_i", [T, GROUPS, TOP], U32)
        top_f = sb("top_f", [T, GROUPS, TOP])
        cand = sb("cand", [T, HEADS, NCAND])
        cand2 = sb("cand2", [T, HEADS, NCAND])
        cand_i = sb("cand_i", [T, HEADS, NCAND])
        fin = sb("fin", [T, HEADS, TOP])
        fin_pos = sb("fin_pos", [T, HEADS, TOP], U32)
        fin_posf = sb("fin_posf", [T, HEADS, TOP])
        picked = sb("picked", [T, HEADS, TOP, NCAND])
        row_f = sb("row_f", [T, HEADS, TOP])
        rows = [sb(f"rows{k}", [T, HEADS, TOP], U32) for k in range(2)]
        shifted = sb("shifted", [T, HEADS, TOP])
        expo = sb("expo", [T, HEADS, TOP])
        esum = sb("esum", [T, HEADS])
        weight = [sb(f"weight{k}", [T, HEADS, TOP]) for k in range(2)]

        kv = sb("kv", [T, HEADS, TOP, 2 * D])
        kk = sb("kk", [T, HEADS, D])
        vv = sb("vv", [T, HEADS, D])
        q_t = sb("q_t", [2 * D, HEADS // 2, T])
        k_t = sb("k_t", [2 * D, HEADS // 2, T])
        sim = sb("sim", [T, HEADS, T])
        nmax = sb("nmax", [T, HEADS])
        prob = sb("prob", [T, HEADS, T])
        psum_row = sb("psum_row", [T, HEADS])
        prow_inv = sb("prow_inv", [T, HEADS])
        prob_t = sb("prob_t", [T, HEADS, T])
        ao = sb("ao", [T, HEADS, D])
        ao_t = sb("ao_t", [2 * D, HEADS // 2, T])
        h2 = sb("h2", [T, D])
        stats_b = sb("stats_b", [T, 6])
        mv_b = sb("mv_b", [T, 2])
        std_b = sb("std_b", [T, 1])
        rstd_b = sb("rstd_b", [T, 1])
        x3 = sb("x3", [T, D])
        x3_t = sb("x3_t", [D + 1, T])
        qk3 = sb("qk3", [D, 2 * T])
        v3 = sb("v3", [T, D + 2])
        nz3 = sb("nz3", [T, 2])
        keep3 = sb("keep3", [T, 1])
        nmax3 = sb("nmax3", [T, 1])
        nmax3s = sb("nmax3s", [T, 1])
        prob3 = sb("prob3", [T, T])
        sum3 = sb("sum3", [T, 1])
        inv3 = sb("inv3", [T, 1])
        prob3_t = sb("prob3_t", [T, T])
        o3 = sb("o3", [T, D])
        o3_t = sb("o3_t", [D + 1, T])
        h3 = sb("h3", [T, D])
        x4 = sb("x4", [T, D])
        x4_t = sb("x4_t", [D + 1, T])
        rh_t = sb("rh_t", [ROUTER + 1, T])
        rmax = sb("rmax", [T, 1])
        rexp = sb("rexp", [T, EXPERTS])
        rsum = sb("rsum", [T, 1])
        rinv = sb("rinv", [T, 1])
        rprob = sb("rprob", [T, 8])
        rtop = sb("rtop", [T, 8])
        rtop_i = sb("rtop_i", [T, 8], U32)
        rtop_f = sb("rtop_f", [T, 8])
        rdiff = sb("rdiff", [T, 1])
        rw = sb("rw", [T, 4])
        gate = [sb(f"gate{k}", [T, EXPERTS]) for k in range(2)]
        e1 = sb("e1", [128, PAIRS * T])
        e2 = sb("e2", [128, PAIRS * T])
        gated = sb("gated", [T, EXPERTS, D])
        moe = sb("moe", [T, D])
        h4 = [sb(f"h4_{k}", [T, D]) for k in range(2)]

        bank = [ctx.enter_context(nc.psum_tensor(f"bank{k}", [128, 512], F32)) for k in range(8)]
        A, B, C, E = bank[0:4]
        ps_scores = [B, C]
        ps_sim = bank[4:6]

        params_landed = sem("params_landed")
        tokens_landed = sem("tokens_landed")
        consts_done = sem("consts_done")
        taps_done = sem("taps_done")
        tokens_ready = sem("tokens_ready")
        tokens_turned = sem("tokens_turned")
        ids_done = sem("ids_done")
        a_ready = sem("a_ready")
        keyprod_ready = sem("keyprod_ready")
        keyprod_taken = sem("keyprod_taken")
        feat_idx_ready = sem("feat_idx_ready")
        featT_ready = sem("featT_ready")
        featT_taken = sem("featT_taken")
        hid_ready = sem("hid_ready")
        hid_taken = sem("hid_taken")
        fused_ready = sem("fused_ready")
        fused_taken = sem("fused_taken")
        var_ready = sem("var_ready")
        std_ready = sem("std_ready")
        xn_ready = sem("xn_ready")
        xT_ready = sem("xT_ready")
        xT_taken = sem("xT_taken")
        uc_ready = sem("uc_ready")
        uT_ready = sem("uT_ready")
        dbc_ready = sem("dbc_ready")
        bc_taken = sem("bc_taken")
        gt_ready = sem("gt_ready")
        abs_ready = sem("abs_ready")
        exp_ready = sem("exp_ready")
        dta_ready = sem("dta_ready")
        decay_ready = sem("decay_ready")
        dtx_ready = sem("dtx_ready")
        drep_ready = sem("drep_ready")
        mt_ready = sem("mt_ready")
        y_ready = sem("y_ready")
        yn_ready = sem("yn_ready")
        ynT_ready = sem("ynT_ready")
        ynT_taken = sem("ynT_taken")
        mix_ready = sem("mix_ready")
        x2_ready = sem("x2_ready")
        x2T_ready = sem("x2T_ready")
        x2T_taken = sem("x2T_taken")
        scores_ready = sem("scores_ready")
        scores_taken = sem("scores_taken")
        rows_ready = sem("rows_ready")
        shift_ready = sem("shift_ready")
        expo_ready = sem("expo_ready")
        kv_used = sem("kv_used")
        kvsum_ready = sem("kvsum_ready")
        q_ready = sem("q_ready")
        q_taken = sem("q_taken")
        kT_ready = sem("kT_ready")
        kT_taken = sem("kT_taken")
        sim_ready = sem("sim_ready")
        max_ready = sem("max_ready")
        prob_ready = sem("prob_ready")
        probT_ready = sem("probT_ready")
        probT_taken_act = sem("probT_taken_act")
        probT_taken_dve = sem("probT_taken_dve")
        ao_ready = sem("ao_ready")
        ao_taken = sem("ao_taken")
        aoT_ready = sem("aoT_ready")
        aoT_taken = sem("aoT_taken")
        ffn_ready = sem("ffn_ready")
        late_var_ready = sem("late_var_ready")
        late_std_ready = sem("late_std_ready")
        x3_ready = sem("x3_ready")
        x3T_ready = sem("x3T_ready")
        x3T_taken = sem("x3T_taken")
        qkv3_ready = sem("qkv3_ready")
        qkv3_taken = sem("qkv3_taken")
        s3_ready = sem("s3_ready")
        max3_ready = sem("max3_ready")
        prob3_ready = sem("prob3_ready")
        p3T_ready = sem("p3T_ready")
        p3T_taken = sem("p3T_taken")
        o3_ready = sem("o3_ready")
        o3_taken = sem("o3_taken")
        o3T_ready = sem("o3T_ready")
        o3T_taken = sem("o3T_taken")
        proj_ready = sem("proj_ready")
        x4_ready = sem("x4_ready")
        x4T_ready = sem("x4T_ready")
        x4T_taken = sem("x4T_taken")
        r1_ready = sem("r1_ready")
        r1_taken = sem("r1_taken")
        logits_ready = sem("logits_ready")
        rmax_ready = sem("rmax_ready")
        rexp_ready = sem("rexp_ready")
        rdiff_ready = sem("rdiff_ready")
        rw_ready = sem("rw_ready")
        e1_ready = sem("e1_ready")
        e1_taken = sem("e1_taken")
        e2_ready = sem("e2_ready")
        e2_taken = sem("e2_taken")
        e3_ready = sem("e3_ready")
        h4_ready = sem("h4_ready")
        feat_landed = [sem(f"feat_landed{k}") for k in range(2)]
        kv_landed = [sem(f"kv_landed{h}") for h in range(HEADS)]
        out_landed = [sem(f"out_landed{k}") for k in range(2)]


        def value(eng, v):
            return v if isinstance(v, int) else eng.compute_val(v)

        def weave(*parts):
            at = {part: next(part, None) for part in parts}
            while any(tick is not None for tick in at.values()):
                part = min((q for q in parts if at[q] is not None), key=lambda q: at[q])
                at[part] = next(part, None)

        def each_sequence(eng, before, sums, after):
            last = SEQS // 2
            weave(before(1, 1, 0))
            weave(before(2, 1, 1), sums(1, 1, 0))
            if SEQS > 2:
                with eng.Fori(0, last - 1) as i:
                    n1, n2, n3, n4 = (eng.snap(i * 2 + c) for c in (1, 2, 3, 4))
                    t1, t2 = (eng.snap(i + c) for c in (1, 2))
                    weave(before(n3, t2, 0), after(n1, t1, 0), sums(n2, t1, 1))
                    weave(before(n4, t2, 1), after(n2, t1, 1), sums(n3, t2, 0))
            weave(after(SEQS - 1, last, 0), sums(SEQS, last, 1))
            weave(after(SEQS, last, 1))

        block = ctx.enter_context(nc.Block())

        @block.sync
        def _(sp):
            sp.dma_start(P[:, :], params).then_inc(params_landed, 16)
            for k in range(2):
                sp.sem_inc(out_landed[k], 16)
            sp.dma_start(tok_i[:, :], tokens).then_inc(tokens_landed, 16)

            def nothing(n, turn, k):
                yield 0

            def after(n, turn, k):
                yield 60
                sp.wait_ge(params_landed, 16)
                sp.wait_ge(h4_ready, n)
                sp.dma_start(out[bass.ds(n - 1, 1), :, :].rearrange("a t d -> (a t) d"), h4[k][:, :]).then_inc(out_landed[k], 16)

            each_sequence(sp, nothing, nothing, after)
            for k in range(2):
                sp.wait_ge(out_landed[k], 16 * (SEQS // 2) + 16)

        @block.gpsimd
        def _(pool):
            def gather_features(n, k):
                count = value(pool, n)
                pool.wait_ge(params_landed, 16)
                pool.wait_ge(feat_idx_ready, count)
                pool.indirect_dma_start(feat[k][:, :], None, feature_table,
                                        bass.IndirectOffsetOnAxis(feat_idx[:, 0:1], 0)).then_inc(feat_landed[k], 16)

            def gather_rows(n, turn, k, ahead=True):
                if ahead:
                    gather_features(n + 1, 1 - k)
                pool.wait_ge(params_landed, 16)
                pool.wait_ge(rows_ready, n)
                for h in range(HEADS):
                    if not (isinstance(n, int) and n == 1):
                        count = value(pool, (n - 2) * HEADS + h + 1)
                        pool.wait_ge(params_landed, 16)
                        pool.wait_ge(kv_used, count)
                    for t in range(TOP):
                        pool.indirect_dma_start(kv[:, h, t, :], None, memory_table,
                                                bass.IndirectOffsetOnAxis(rows[k][:, h, t:t + 1], 0)
                                                ).then_inc(kv_landed[h], 16)

            gather_features(1, 0)
            gather_rows(1, 1, 0)
            if SEQS > 2:
                with pool.Fori(0, SEQS // 2 - 1) as i:
                    n2, n3 = (pool.snap(i * 2 + c) for c in (2, 3))
                    gather_rows(n2, None, 1)
                    gather_rows(n3, None, 0)
            gather_rows(SEQS, None, 1, ahead=False)

        @block.scalar
        def _(act):
            def root(tick, var, std_, sem_in, sem_out, count):
                yield tick
                count = value(act, count)
                act.wait_ge(params_landed, 16)
                act.wait_ge(sem_in, count)
                nc.scalar.activation(std_, var, ACT.Sqrt, bias=eps_col[0:T, :]).then_inc(sem_out, 1)

            def copy(o, i):
                return nc.scalar.activation(o, i, ACT.Copy)

            act.wait_ge(params_landed, 16)
            nc.scalar.activation(neg_a[:, :], par("a_log"), ACT.Exp).then_inc(a_ready, 1)
            for s in range(2):
                act.wait_ge(keyprod_ready, s + 1)
                copy(w_scores[:, s * 512:(s + 1) * 512], [A, B][s][0:D, :]).then_inc(keyprod_taken, 1)
            act.wait_ge(consts_done, 1)

            def before(n, turn, k):
                yield 2
                act.wait_ge(params_landed, 16)
                act.wait_ge(featT_ready, n)
                copy(ig_t[:, :], A[:, 0:T])
                copy(visit_t[:, :], A[0:VISIT, T:2 * T]).then_inc(featT_taken, 1)
                yield 4
                act.wait_ge(params_landed, 16)
                act.wait_ge(hid_ready, n)
                nc.scalar.activation(igh_t[:, :], A[:, 256:384], ACT.Gelu, bias=par("b_ig"))
                nc.scalar.activation(vh_t[0:D, :], A[0:D, 384:512], ACT.Gelu, bias=par("b_visit")).then_inc(hid_taken, 1)
                yield 6
                act.wait_ge(params_landed, 16)
                act.wait_ge(fused_ready, n)
                nc.scalar.activation(fused[:, :], B[:, 0:D], ACT.Gelu).then_inc(fused_taken, 1)
                for j in range(3):
                    yield from root(8 + 2 * j, mv[:, 1:2], std[:, :], var_ready, std_ready, (n - 1) * 5 + j + 1)
                yield 17
                act.wait_ge(params_landed, 16)
                act.wait_ge(uc_ready, n)
                nc.scalar.activation(u_t[:, :], B[:, 192:320], ACT.Gelu, bias=par("conv_b")).then_inc(uT_ready, 1)
                yield 19
                act.wait_ge(params_landed, 16)
                act.wait_ge(dbc_ready, n)
                copy(bc_t[:, :], C[0:STATE, 0:2 * T]).then_inc(bc_taken, 1)
                yield 20
                act.wait_ge(params_landed, 16)
                act.wait_ge(abs_ready, n)
                nc.scalar.activation(ez[:, :], absz[:, :], ACT.Exp, scale=-1.0).then_inc(exp_ready, 1)
                yield 22
                act.wait_ge(params_landed, 16)
                act.wait_ge(dta_ready, n)
                nc.scalar.activation(decay[:, :], dt_a[:, :], ACT.Exp, scale=-1.0).then_inc(decay_ready, 1)
                for h in range(SSM_HEADS):
                    ins = nc.scalar.activation(dtx[:, h * D:(h + 1) * D], C[:, 256 + h * D:256 + (h + 1) * D],
                                               ACT.Copy, scale=dt_[:, h:h + 1])
                ins.then_inc(dtx_ready, 1)
                for j in range(3, 5):
                    yield from root(27 if j == 3 else 33, mv[:, 1:2], std[:, :], var_ready, std_ready, (n - 1) * 5 + j + 1)
                yield 38
                act.wait_ge(params_landed, 16)
                act.wait_ge(scores_ready, n)
                for s in range(2):
                    ins = copy(scores[:, s * HEADS:(s + 1) * HEADS, :].rearrange("p g k -> p (g k)"), ps_scores[s][:, :])
                ins.then_inc(scores_taken, 1)
                yield 57
                act.wait_ge(params_landed, 16)
                act.wait_ge(shift_ready, n)
                nc.scalar.activation(expo[:, :, :], shifted[:, :, :], ACT.Exp).then_inc(expo_ready, 1)

            def after(n, turn, k):
                yield 1.5
                act.wait_ge(params_landed, 16)
                act.wait_ge(q_ready, n)
                copy(q_t[:, :, :].rearrange("p a t -> p (a t)"), bank[7][:, :]).then_inc(q_taken, 1)
                yield 2
                act.wait_ge(params_landed, 16)
                act.wait_ge(kT_ready, n)
                copy(k_t[:, :, :].rearrange("p a t -> p (a t)"), bank[6][:, :]).then_inc(kT_taken, 1)
                yield 7
                act.wait_ge(params_landed, 16)
                act.wait_ge(max_ready, n)
                for h in range(HEADS):
                    ins = nc.scalar.activation(prob[:, h, :], sim[:, h, :], ACT.Exp, bias=nmax[:, h:h + 1],
                                               accum_out=psum_row[:, h:h + 1])
                ins.then_inc(prob_ready, 1)
                yield 11
                act.wait_ge(params_landed, 16)
                act.wait_ge(probT_ready, n)
                copy(prob_t[:, 0:4, :].rearrange("p a t -> p (a t)"), bank[6][:, :]).then_inc(probT_taken_act, 1)
                yield 15
                act.wait_ge(params_landed, 16)
                act.wait_ge(aoT_ready, n)
                copy(ao_t[:, :, :].rearrange("p a t -> p (a t)"), bank[5][:, :]).then_inc(aoT_taken, 1)
                yield from root(18, mv_b[:, 1:2], std_b[:, :], late_var_ready, late_std_ready, (n - 1) * 2 + 1)
                yield 21
                act.wait_ge(params_landed, 16)
                act.wait_ge(x3T_ready, n)
                copy(x3_t[0:D, :], bank[4][0:D, 0:T]).then_inc(x3T_taken, 1)
                yield 23
                act.wait_ge(params_landed, 16)
                act.wait_ge(qkv3_ready, n)
                copy(qk3[:, :], bank[4][0:D, T:3 * T])
                copy(v3[:, :], bank[4][:, 3 * T:3 * T + D + 2]).then_inc(qkv3_taken, 1)
                yield 26
                act.wait_ge(params_landed, 16)
                act.wait_ge(max3_ready, n)
                nc.scalar.activation(prob3[:, :], bank[5][:, 0:T], ACT.Exp, bias=nmax3s[:, :], scale=D ** -0.5,
                                     accum_out=sum3[:, :]).then_inc(prob3_ready, 1)
                yield 28
                act.wait_ge(params_landed, 16)
                act.wait_ge(p3T_ready, n)
                copy(prob3_t[:, :], bank[5][:, T:2 * T]).then_inc(p3T_taken, 1)
                yield 32
                act.wait_ge(params_landed, 16)
                act.wait_ge(o3T_ready, n)
                copy(o3_t[0:D, :], bank[5][0:D, 320:320 + T]).then_inc(o3T_taken, 1)
                yield from root(35, mv_b[:, 1:2], std_b[:, :], late_var_ready, late_std_ready, (n - 1) * 2 + 2)
                yield 38
                act.wait_ge(params_landed, 16)
                act.wait_ge(x4T_ready, n)
                copy(x4_t[0:D, :], bank[6][0:D, 0:T]).then_inc(x4T_taken, 1)
                yield 40
                act.wait_ge(params_landed, 16)
                act.wait_ge(r1_ready, n)
                nc.scalar.activation(rh_t[0:ROUTER, :], bank[6][0:ROUTER, T:2 * T], ACT.Relu).then_inc(r1_taken, 1)
                yield 40
                act.wait_ge(params_landed, 16)
                act.wait_ge(e1_ready, n)
                nc.scalar.activation(e1[:, :], bank[7][:, 0:PAIRS * T], ACT.Relu).then_inc(e1_taken, 1)
                yield 43
                act.wait_ge(params_landed, 16)
                act.wait_ge(rmax_ready, n)
                nc.scalar.activation(rexp[:, :], bank[6][:, 256:256 + EXPERTS], ACT.Exp, bias=rmax[:, :],
                                     accum_out=rsum[:, :]).then_inc(rexp_ready, 1)
                yield 43.5
                act.wait_ge(params_landed, 16)
                act.wait_ge(e2_ready, n)
                for j in range(PAIRS):
                    ins = nc.scalar.activation(e2[:, j * T:(j + 1) * T], bank[4][:, j * T:(j + 1) * T], ACT.Relu,
                                               bias=par("e_b2")[:, j:j + 1])
                ins.then_inc(e2_taken, 1)
                yield 45
                act.wait_ge(params_landed, 16)
                act.wait_ge(rdiff_ready, n)
                nc.scalar.activation(rw[:, 0:1], rdiff[:, :], ACT.Exp).then_inc(rw_ready, 1)

            def nothing(n, turn, k):
                yield 0

            each_sequence(act, before, nothing, after)

        @block.tensor
        def _(pe):
            mm = nc.tensor.matmul
            ident = par("ident")

            pe.wait_ge(params_landed, 16)
            for s in range(2):
                for h in range(HEADS):
                    g = s * HEADS + h
                    ins = mm([A, B][s][0:D, h * KEYS:(h + 1) * KEYS], par("wq_pk_t")[:, g * D:(g + 1) * D],
                             par("pk_keys_t")[:, g * KEYS:(g + 1) * KEYS], start=True, stop=True)
                ins.then_inc(keyprod_ready, 1)
            pe.wait_ge(tokens_ready, 1)
            nc.tensor.transpose(C[0:T, 0:SEQS], tok_clip[:, :], ident[0:SEQS, 0:SEQS])
            nc.tensor.transpose(C[0:T, 128:128 + SEQS], tok_ok[:, :], ident[0:SEQS, 0:SEQS]).then_inc(tokens_turned, 1)
            pe.wait_ge(keyprod_taken, 2)
            pe.wait_ge(ids_done, 1)
            pe.wait_ge(taps_done, 1)
            pe.wait_ge(consts_done, 1)

            def before(n, turn, k):
                yield 1
                count = value(pe, turn * 16)
                pe.wait_ge(params_landed, 16)
                pe.wait_ge(feat_landed[k], count)
                nc.tensor.transpose(A[:, 0:T], feat[k][:, 0:ITEM + GEO], ident)
                nc.tensor.transpose(A[0:VISIT, T:2 * T], feat[k][:, ITEM + GEO:FEAT], ident).then_inc(featT_ready, 1)
                yield 3
                pe.wait_ge(params_landed, 16)
                pe.wait_ge(featT_taken, n)
                mm(A[:, 256:384], par("w_ig"), ig_t[:, :], start=True, stop=True)
                mm(A[0:D, 384:512], par("w_visit"), visit_t[:, :], start=True, stop=True).then_inc(hid_ready, 1)
                yield 5
                pe.wait_ge(params_landed, 16)
                pe.wait_ge(hid_taken, n)
                mm(B[:, 0:D], igh_t[:, :], par("w_fuse_ig"), start=True, stop=False)
                mm(B[:, 0:D], vh_t[:, :], par("w_fuse_v"), start=False, stop=True).then_inc(fused_ready, 1)
                yield 14
                pe.wait_ge(params_landed, 16)
                pe.wait_ge(xn_ready, n)
                nc.tensor.transpose(B[0:D, 64:64 + T], xn[:, :], ident).then_inc(xT_ready, 1)
                yield 16
                pe.wait_ge(params_landed, 16)
                pe.wait_ge(xT_taken, n)
                for j in range(3):
                    ins = mm(B[:, 192:320], w_tap[:, j, :], x_t[:, j:j + T], start=(j == 0), stop=(j == 2))
                ins.then_inc(uc_ready, 1)
                yield 18
                pe.wait_ge(params_landed, 16)
                pe.wait_ge(uT_ready, n)
                mm(B[:, 320:320 + SSM_HEADS], u_t[:, :], par("w_xproj")[:, 0:SSM_HEADS], start=True, stop=True)
                for j in range(2):
                    mm(C[0:STATE, j * T:(j + 1) * T], par("w_xproj")[:, SSM_HEADS + j * STATE:SSM_HEADS + (j + 1) * STATE],
                       u_t[:, :], start=True, stop=True)
                nc.tensor.transpose(C[:, 256:384], u_t[:, :], ident).then_inc(dbc_ready, 1)
                yield 20
                pe.wait_ge(params_landed, 16)
                pe.wait_ge(bc_taken, n)
                mm(E[:, 256:384], bc_t[:, 0:T], bc_t[:, T:2 * T], start=True, stop=True).then_inc(gt_ready, 1)
                yield 23
                pe.wait_ge(params_landed, 16)
                pe.wait_ge(decay_ready, n)
                for h in range(SSM_HEADS):
                    ins = mm(E[:, h * T:(h + 1) * T], decay[:, h:h + 1].to_broadcast([T, T]), ident, start=True, stop=True)
                ins.then_inc(drep_ready, 1)
                yield 25
                pe.wait_ge(params_landed, 16)
                pe.wait_ge(mt_ready, n)
                pe.wait_ge(dtx_ready, n)
                for h in range(SSM_HEADS):
                    c = slice(h * D, (h + 1) * D)
                    o = E[:, 384 + h * D:384 + (h + 1) * D]
                    mm(o, u_t[:, :], skip_diag[:, c], start=True, stop=False)
                    ins = mm(o, m_t[:, h, :], dtx[:, c], start=False, stop=True)
                ins.then_inc(y_ready, 1)
                yield 29
                pe.wait_ge(params_landed, 16)
                pe.wait_ge(yn_ready, n)
                nc.tensor.transpose(A[:, 0:T], yn[:, :], ident).then_inc(ynT_ready, 1)
                yield 31
                pe.wait_ge(params_landed, 16)
                pe.wait_ge(ynT_taken, n)
                mm(A[:, 128:128 + D], yn_t[:, :], par("w_out"), start=True, stop=True).then_inc(mix_ready, 1)
                yield 35
                pe.wait_ge(params_landed, 16)
                pe.wait_ge(x2_ready, n)
                nc.tensor.transpose(A[0:D, 192:192 + T], x2[:, :], ident).then_inc(x2T_ready, 1)
                yield 37
                pe.wait_ge(params_landed, 16)
                pe.wait_ge(x2T_taken, n)
                for s in range(2):
                    ins = mm(ps_scores[s][:, :], x2_t[k][:, :], w_scores[:, s * 512:(s + 1) * 512], start=True, stop=True)
                ins.then_inc(scores_ready, 1)

            def after(n, turn, k):
                yield 1
                for a in range(HEADS // 2):
                    ins = mm(bank[7][:, a * T:(a + 1) * T], par("wq")[:, a * 128:(a + 1) * 128], x2_t[k][:, :],
                             start=True, stop=True)
                ins.then_inc(q_ready, 1)
                yield 1
                pe.wait_ge(params_landed, 16)
                pe.wait_ge(kvsum_ready, n)
                for a in range(HEADS // 2):
                    ins = nc.tensor.transpose(bank[6][:, a * T:(a + 1) * T],
                                              kk[:, 2 * a:2 * a + 2, :].rearrange("p h d -> p (h d)"), ident)
                ins.then_inc(kT_ready, 1)
                yield 3
                pe.wait_ge(params_landed, 16)
                pe.wait_ge(q_taken, n)
                pe.wait_ge(kT_taken, n)
                for h in range(HEADS):
                    r = (h % 2) * D
                    ins = mm(ps_sim[h % 2][:, (h // 2) * T:(h // 2 + 1) * T], q_t[r:r + D, h // 2, :],
                             k_t[r:r + D, h // 2, :], start=True, stop=True)
                ins.then_inc(sim_ready, 1)
                yield 10
                pe.wait_ge(params_landed, 16)
                pe.wait_ge(prob_ready, n)
                for h in range(HEADS):
                    ins = nc.tensor.transpose(bank[6 + h // 4][:, (h % 4) * T:(h % 4 + 1) * T], prob[:, h, :], ident)
                ins.then_inc(probT_ready, 1)
                yield 12
                pe.wait_ge(params_landed, 16)
                pe.wait_ge(probT_taken_act, n)
                pe.wait_ge(probT_taken_dve, n)
                for h in range(HEADS):
                    ins = mm(bank[4][:, h * D:(h + 1) * D], prob_t[:, h, :], vv[:, h, :], start=True, stop=True)
                ins.then_inc(ao_ready, 1)
                yield 14
                pe.wait_ge(params_landed, 16)
                pe.wait_ge(ao_taken, n)
                for a in range(HEADS // 2):
                    ins = nc.tensor.transpose(bank[5][:, a * T:(a + 1) * T],
                                              ao[:, 2 * a:2 * a + 2, :].rearrange("p h d -> p (h d)"), ident)
                ins.then_inc(aoT_ready, 1)
                yield 16
                pe.wait_ge(params_landed, 16)
                pe.wait_ge(aoT_taken, n)
                for a in range(HEADS // 2):
                    ins = mm(bank[6][:, 0:D], ao_t[:, a, :], par("wo")[:, a * D:(a + 1) * D],
                             start=(a == 0), stop=(a == HEADS // 2 - 1))
                ins.then_inc(ffn_ready, 1)
                yield 20
                pe.wait_ge(params_landed, 16)
                pe.wait_ge(x3_ready, n)
                nc.tensor.transpose(bank[4][0:D, 0:T], x3[:, :], ident).then_inc(x3T_ready, 1)
                yield 22
                pe.wait_ge(params_landed, 16)
                pe.wait_ge(x3T_taken, n)
                mm(bank[4][0:D, T:2 * T], par("a_q"), x3_t[:, :], start=True, stop=True)
                mm(bank[4][0:D, 2 * T:3 * T], par("a_k"), x3_t[:, :], start=True, stop=True)
                mm(bank[4][:, 3 * T:3 * T + D + 2], x3_t[:, :], par("a_v"), start=True, stop=True).then_inc(qkv3_ready, 1)
                yield 24
                pe.wait_ge(params_landed, 16)
                pe.wait_ge(qkv3_taken, n)
                mm(bank[5][:, 0:T], qk3[:, 0:T], qk3[:, T:2 * T], start=True, stop=True).then_inc(s3_ready, 1)
                yield 27
                pe.wait_ge(params_landed, 16)
                pe.wait_ge(prob3_ready, n)
                nc.tensor.transpose(bank[5][:, T:2 * T], prob3[:, :], ident).then_inc(p3T_ready, 1)
                yield 29
                pe.wait_ge(params_landed, 16)
                pe.wait_ge(p3T_taken, n)
                mm(bank[5][:, 256:256 + D], prob3_t[:, :], v3[:, 0:D], start=True, stop=True).then_inc(o3_ready, 1)
                yield 31
                pe.wait_ge(params_landed, 16)
                pe.wait_ge(o3_taken, n)
                nc.tensor.transpose(bank[5][0:D, 320:320 + T], o3[:, :], ident).then_inc(o3T_ready, 1)
                yield 33
                pe.wait_ge(params_landed, 16)
                pe.wait_ge(o3T_taken, n)
                mm(bank[5][:, 448:448 + D], o3_t[:, :], par("a_o"), start=True, stop=True).then_inc(proj_ready, 1)
                yield 37
                pe.wait_ge(params_landed, 16)
                pe.wait_ge(x4_ready, n)
                nc.tensor.transpose(bank[6][0:D, 0:T], x4[:, :], ident).then_inc(x4T_ready, 1)
                yield 39
                pe.wait_ge(params_landed, 16)
                pe.wait_ge(x4T_taken, n)
                mm(bank[6][0:ROUTER, T:2 * T], par("r_w1"), x4_t[:, :], start=True, stop=True).then_inc(r1_ready, 1)
                for j in range(PAIRS):
                    ins = mm(bank[7][:, j * T:(j + 1) * T], par("e_w1")[:, j * 128:(j + 1) * 128], x4_t[:, :],
                             start=True, stop=True)
                ins.then_inc(e1_ready, 1)
                yield 41
                pe.wait_ge(params_landed, 16)
                pe.wait_ge(r1_taken, n)
                mm(bank[6][:, 256:256 + EXPERTS], rh_t[:, :], par("r_w2"), start=True, stop=True).then_inc(logits_ready, 1)
                yield 41
                pe.wait_ge(params_landed, 16)
                pe.wait_ge(e1_taken, n)
                for j in range(PAIRS):
                    ins = mm(bank[4][:, j * T:(j + 1) * T], par("e_w2")[:, j * 128:(j + 1) * 128],
                             e1[:, j * T:(j + 1) * T], start=True, stop=True)
                ins.then_inc(e2_ready, 1)
                yield 44
                pe.wait_ge(params_landed, 16)
                pe.wait_ge(e2_taken, n)
                for j in range(PAIRS):
                    c = slice(j * 128, (j + 1) * 128)
                    mm(bank[5][:, c], e2[:, j * T:(j + 1) * T], par("e_w3")[:, c], start=True, stop=False)
                    ins = mm(bank[5][:, c], par("ones_row"), par("e_b3")[:, c], start=False, stop=True)
                ins.then_inc(e3_ready, 1)

            def nothing(n, turn, k):
                yield 0

            each_sequence(pe, before, nothing, after)

        @block.vector
        def _(dve):
            V = nc.vector

            def done():
                dve.drain()

            def normalize(tick, o, x, late, count, signal):
                if late:
                    st, m, sd, rs = stats_b, mv_b, std_b, rstd_b
                    var_sem, std_sem = late_var_ready, late_std_ready
                else:
                    st, m, sd, rs = stats, mv, std, rstd
                    var_sem, std_sem = var_ready, std_ready
                V.bn_stats(st[:, :], x)
                done()
                V.bn_aggr(m[:, :], st[:, :]).then_inc(var_sem, 1)
                yield tick
                count = value(dve, count)
                dve.wait_ge(params_landed, 16)
                dve.wait_ge(std_sem, count)
                V.reciprocal(rs[:, :], sd[:, :])
                done()
                ins = V.tensor_scalar(o, x, m[:, 0:1], rs[:, :], ALU.subtract, ALU.mult)
                if signal is not None:
                    ins.then_inc(signal, 1)

            for x, v in ((eps_col[:, :], EPS), (zero_col[:, :], 0.0), (x_t[:, 0:1], 0.0), (x_t[:, T + 1:T + 2], 0.0),
                         (vh_t[D:D + 1, :], 1.0), (x3_t[D:D + 1, :], 1.0), (o3_t[D:D + 1, :], 1.0),
                         (x4_t[D:D + 1, :], 1.0), (rh_t[ROUTER:ROUTER + 1, :], 1.0), (rprob[:, :], -1.0)):
                ins = V.memset(x, v)
            ins.then_inc(consts_done, 1)
            dve.wait_ge(params_landed, 16)
            V.tensor_scalar(skip_diag[:, :], par("ident"), par("d_skip"), None, ALU.mult)
            for j in range(3):
                ins = V.tensor_tensor(w_tap[:, j, :], par("w_in"), par("conv_w")[:, j * CH:(j + 1) * CH], ALU.mult)
            ins.then_inc(taps_done, 1)
            dve.wait_ge(tokens_landed, 16)
            V.tensor_copy(tok_f[:, :], tok_i[:, :])
            done()
            V.tensor_scalar(tok_ok[:, :], tok_f[:, :], 0.0, 0.1, ALU.not_equal, ALU.mult)
            V.tensor_scalar(tok_clip[:, :], tok_f[:, :], 0.0, float(LAST_ITEM), ALU.max, ALU.min).then_inc(tokens_ready, 1)
            dve.wait_ge(tokens_turned, 1)
            V.tensor_copy(ids_t[:, 0:SEQS], C[0:T, 0:SEQS])
            V.tensor_copy(ids_t[:, SEQS:SEQS + 1], C[0:T, 0:1])
            V.tensor_copy(ok_t[:, :], C[0:T, 128:128 + SEQS]).then_inc(ids_done, 1)
            done()
            V.tensor_copy(feat_idx[:, :], ids_t[:, 0:1]).then_inc(feat_idx_ready, 1)
            dve.wait_ge(a_ready, 1)

            def top16(tick, step, values, spare, tops, places):
                n = values.shape[1]
                for g in range(n):
                    V.max(tops[:, g, 0:8], values[:, g, :])
                done()
                yield tick + step
                for g in range(n):
                    V.match_replace(spare[:, g, :], tops[:, g, 0:8], values[:, g, :], LOWEST)
                for g in range(n):
                    V.max_index(places[:, g, 0:8], tops[:, g, 0:8], values[:, g, :])
                done()
                yield tick + 3 * step
                for g in range(n):
                    V.max(tops[:, g, 8:16], spare[:, g, :])
                done()
                yield tick + 4 * step
                for g in range(n):
                    V.max_index(places[:, g, 8:16], tops[:, g, 8:16], spare[:, g, :])
                done()

            def before(n, turn, k):
                yield 1
                count = value(dve, turn * 16)
                dve.wait_ge(params_landed, 16)
                dve.wait_ge(feat_landed[k], count)
                V.tensor_copy(feat_idx[:, :], ids_t[:, bass.ds(n, 1)]).then_inc(feat_idx_ready, 1)
                V.tensor_copy(tok_mask[:, :], ok_t[:, bass.ds(n - 1, 1)])
                yield 7
                dve.wait_ge(params_landed, 16)
                dve.wait_ge(fused_taken, n)
                c = (n - 1) * 5
                yield from normalize(9, tmp[0][:, :], fused[:, :], False, c + 1, None)
                done()
                V.tensor_tensor(tmp[1][:, :], tmp[0][:, :], par("gamma"), ALU.mult)
                done()
                V.tensor_tensor(tmp[0][:, :], tmp[1][:, :], par("beta"), ALU.add)
                done()
                V.scalar_tensor_tensor(h0[:, :], tmp[0][:, :], tok_mask[:, :], feat[k][:, 0:D], ALU.mult, ALU.add)
                done()
                yield from normalize(11, src[:, :], h0[:, :], False, c + 2, None)
                done()
                yield from normalize(13, xn[:, :], src[:, :], False, c + 3, xn_ready)
                V.tensor_tensor(h0s[:, :], h0[:, :], src[:, :], ALU.add)
                yield 15
                dve.wait_ge(params_landed, 16)
                dve.wait_ge(xT_ready, n)
                V.tensor_scalar(x_t[:, 1:T + 1], B[0:D, 64:64 + T], par("ln_w"), par("ln_b"), ALU.mult, ALU.add).then_inc(xT_taken, 1)
                yield 19
                dve.wait_ge(params_landed, 16)
                dve.wait_ge(dbc_ready, n)
                V.tensor_tensor(z[:, :], B[:, 320:320 + SSM_HEADS], par("dt_bias"), ALU.add)
                done()
                V.scalar_tensor_tensor(absz[:, :], z[:, :], -1.0, z[:, :], ALU.mult, ALU.max).then_inc(abs_ready, 1)
                yield 21
                dve.wait_ge(params_landed, 16)
                dve.wait_ge(exp_ready, n)
                V.tensor_scalar(den[:, :], ez[:, :], 2.0, None, ALU.add)
                done()
                V.reciprocal(absz[:, :], den[:, :])
                done()
                V.tensor_tensor(s_at[:, :], ez[:, :], absz[:, :], ALU.mult)
                done()
                V.tensor_tensor(s_sq[:, :], s_at[:, :], s_at[:, :], ALU.mult)
                done()
                V.tensor_scalar(poly[0][:, :], s_sq[:, :], 1.0 / (2 * LOG1P_TERMS + 1), None, ALU.mult)
                at = 0
                for j in range(LOG1P_TERMS - 1, 0, -1):
                    done()
                    V.scalar_tensor_tensor(poly[1 - at][:, :], poly[at][:, :], 1.0 / (2 * j + 1), s_sq[:, :], ALU.add, ALU.mult)
                    at = 1 - at
                done()
                V.scalar_tensor_tensor(poly[1 - at][:, :], poly[at][:, :], 1.0, s_at[:, :], ALU.add, ALU.mult)
                V.tensor_scalar(den[:, :], z[:, :], 0.0, None, ALU.max)
                done()
                V.scalar_tensor_tensor(dt_[:, :], poly[1 - at][:, :], 2.0, den[:, :], ALU.mult, ALU.add)
                done()
                V.tensor_tensor(dt_a[:, :], dt_[:, :], neg_a[:, :], ALU.mult).then_inc(dta_ready, 1)
                yield 24
                dve.wait_ge(params_landed, 16)
                dve.wait_ge(drep_ready, n)
                for h in range(SSM_HEADS):
                    V.tensor_tensor_scan(l_t[:, h, :], E[:, h * T:(h + 1) * T], par("ident"), 0.0, ALU.mult, ALU.add)
                dve.wait_ge(params_landed, 16)
                dve.wait_ge(gt_ready, n)
                done()
                for h in range(SSM_HEADS):
                    ins = V.tensor_tensor(m_t[:, h, :], E[:, 256:384], l_t[:, h, :], ALU.mult)
                ins.then_inc(mt_ready, 1)
                yield 26
                dve.wait_ge(params_landed, 16)
                dve.wait_ge(y_ready, n)
                yield from normalize(28, yn[:, :], E[:, 384:512], False, c + 4, yn_ready)
                yield 30
                dve.wait_ge(params_landed, 16)
                dve.wait_ge(ynT_ready, n)
                V.tensor_scalar(yn_t[:, :], A[:, 0:T], par("oln_w"), par("oln_b"), ALU.mult, ALU.add).then_inc(ynT_taken, 1)
                yield 32
                dve.wait_ge(params_landed, 16)
                dve.wait_ge(mix_ready, n)
                V.tensor_tensor(h1[k][:, :], A[:, 128:128 + D], h0s[:, :], ALU.add)
                done()
                yield from normalize(34, x2[:, :], h1[k][:, :], False, c + 5, x2_ready)
                yield 36
                dve.wait_ge(params_landed, 16)
                dve.wait_ge(x2T_ready, n)
                V.tensor_copy(x2_t[k][:, :], A[0:D, 192:192 + T]).then_inc(x2T_taken, 1)
                yield 39
                dve.wait_ge(params_landed, 16)
                dve.wait_ge(scores_taken, n)
                yield from top16(39, 2, scores, scores2, top_s, top_i)
                yield 49
                V.tensor_copy(top_f[:, :, :], top_i[:, :, :])
                done()
                V.scalar_tensor_tensor(top_f[:, HEADS:GROUPS, :].rearrange("p h k -> p (h k)"),
                                       top_f[:, HEADS:GROUPS, :].rearrange("p h k -> p (h k)"), float(KEYS),
                                       par("head_offset"), ALU.mult, ALU.add)
                done()
                at = 0
                for first, ranks, partners in CAND_BLOCKS:
                    shape = [T, HEADS, ranks, partners]
                    for of, o in ((top_s, cand), (top_f, cand_i)):
                        V.tensor_tensor(o[:, :, at:at + ranks * partners].rearrange("p h (a b) -> p h a b", a=ranks),
                                        of[:, 0:HEADS, first:first + ranks].unsqueeze(3).to_broadcast(shape),
                                        of[:, HEADS:GROUPS, 0:partners].unsqueeze(2).to_broadcast(shape), ALU.add)
                    at += ranks * partners
                done()
                yield from top16(51, 1, cand, cand2, fin, fin_pos)
                yield 56
                V.tensor_copy(fin_posf[:, :, :], fin_pos[:, :, :])
                V.tensor_tensor(shifted[:, :, :], fin[:, :, :], fin[:, :, 0:1].to_broadcast([T, HEADS, TOP]),
                                ALU.subtract).then_inc(shift_ready, 1)
                done()
                yield 58
                shape = [T, HEADS, TOP, NCAND]
                flat = [T, HEADS * TOP, NCAND]
                V.tensor_tensor(picked[:, :, :, :].rearrange("p h k c -> p (h k) c"),
                                fin_posf[:, :, :].rearrange("p h k -> p (h k)").unsqueeze(2).to_broadcast(flat),
                                par("iota_cand").unsqueeze(1).to_broadcast(flat), ALU.is_equal)
                done()
                yield 65
                V.tensor_tensor(picked[:, :, :, :], picked[:, :, :, :],
                                cand_i[:, :, :].unsqueeze(2).to_broadcast(shape), ALU.mult)
                done()
                yield 71
                V.tensor_reduce(row_f[:, :, :], picked[:, :, :, :], AX.X, ALU.add)
                done()
                V.tensor_copy(rows[k][:, :, :], row_f[:, :, :]).then_inc(rows_ready, 1)
                yield 77
                dve.wait_ge(params_landed, 16)
                dve.wait_ge(expo_ready, n)
                V.tensor_reduce(esum[:, :], expo[:, :, :], AX.X, ALU.add)
                done()
                V.reciprocal(esum[:, :], esum[:, :])
                done()
                V.tensor_tensor(weight[k][:, :, :], expo[:, :, :], esum[:, :].unsqueeze(2).to_broadcast([T, HEADS, TOP]), ALU.mult)

            def sums(n, turn, k):
                for h in range(HEADS):
                    yield 18 + 14 * h
                    count = value(dve, n * TOP * 16)
                    dve.wait_ge(params_landed, 16)
                    dve.wait_ge(kv_landed[h], count)
                    V.tensor_tensor(kv[:, h, :, :], kv[:, h, :, :],
                                    weight[k][:, h, :].unsqueeze(2).to_broadcast([T, TOP, 2 * D]), ALU.mult)
                    done()
                    V.tensor_reduce(kk[:, h, :], kv[:, h, :, 0:D].rearrange("p k d -> p d k"), AX.X, ALU.add)
                    ins = V.tensor_reduce(vv[:, h, :], kv[:, h, :, D:2 * D].rearrange("p k d -> p d k"), AX.X, ALU.add)
                    ins.then_inc(kv_used, 1)
                done()
                dve.sem_inc(kvsum_ready, 1)

            def after(n, turn, k):
                yield 4
                dve.wait_ge(params_landed, 16)
                dve.wait_ge(sim_ready, n)
                for a in range(2):
                    V.scalar_tensor_tensor(sim[:, a:HEADS:2, :], ps_sim[a][:, :].rearrange("p (h t) -> p h t", h=4), D ** -0.5,
                                           par("causal").unsqueeze(1).to_broadcast([T, 4, T]), ALU.mult, ALU.add)
                done()
                V.tensor_reduce(nmax[:, :], sim[:, :, :], AX.X, ALU.max, negate=True).then_inc(max_ready, 1)
                yield 10.5
                dve.wait_ge(params_landed, 16)
                dve.wait_ge(prob_ready, n)
                V.reciprocal(prow_inv[:, :], psum_row[:, :])
                yield 11
                dve.wait_ge(params_landed, 16)
                dve.wait_ge(probT_ready, n)
                V.tensor_copy(prob_t[:, 4:8, :].rearrange("p a t -> p (a t)"), bank[7][:, :]).then_inc(probT_taken_dve, 1)
                yield 13
                dve.wait_ge(params_landed, 16)
                dve.wait_ge(ao_ready, n)
                V.tensor_tensor(ao[:, :, :], bank[4][:, :].rearrange("p (h d) -> p h d", h=HEADS),
                                prow_inv[:, :].unsqueeze(2).to_broadcast([T, HEADS, D]), ALU.mult).then_inc(ao_taken, 1)
                yield 17
                dve.wait_ge(params_landed, 16)
                dve.wait_ge(ffn_ready, n)
                V.tensor_tensor(h2[:, :], bank[6][:, 0:D], h1[k][:, :], ALU.add)
                done()
                c = (n - 1) * 2
                yield from normalize(19, x3[:, :], h2[:, :], True, c + 1, x3_ready)
                yield 25
                dve.wait_ge(params_landed, 16)
                dve.wait_ge(s3_ready, n)
                V.tensor_reduce(nmax3[:, :], bank[5][:, 0:T], AX.X, ALU.max, negate=True)
                V.tensor_scalar(nz3[:, :], v3[:, D:D + 2], 0.0, None, ALU.not_equal)
                done()
                V.tensor_scalar(nmax3s[:, :], nmax3[:, :], D ** -0.5, None, ALU.mult).then_inc(max3_ready, 1)
                V.tensor_tensor(keep3[:, :], nz3[:, 0:1], nz3[:, 1:2], ALU.mult)
                yield 27
                dve.wait_ge(params_landed, 16)
                dve.wait_ge(prob3_ready, n)
                V.reciprocal(inv3[:, :], sum3[:, :])
                yield 30
                dve.wait_ge(params_landed, 16)
                dve.wait_ge(o3_ready, n)
                done()
                V.tensor_scalar(o3[:, :], bank[5][:, 256:256 + D], inv3[:, :], keep3[:, :], ALU.mult, ALU.mult).then_inc(o3_taken, 1)
                yield 34
                dve.wait_ge(params_landed, 16)
                dve.wait_ge(proj_ready, n)
                V.tensor_tensor(h3[:, :], bank[5][:, 448:448 + D], h2[:, :], ALU.add)
                done()
                yield from normalize(36, x4[:, :], h3[:, :], True, c + 2, x4_ready)
                yield 42
                dve.wait_ge(params_landed, 16)
                dve.wait_ge(logits_ready, n)
                V.tensor_reduce(rmax[:, :], bank[6][:, 256:256 + EXPERTS], AX.X, ALU.max, negate=True).then_inc(rmax_ready, 1)
                yield 44
                dve.wait_ge(params_landed, 16)
                dve.wait_ge(rexp_ready, n)
                V.reciprocal(rinv[:, :], rsum[:, :])
                done()
                V.tensor_scalar(rprob[:, 0:EXPERTS], rexp[:, :], rinv[:, :], None, ALU.mult)
                done()
                V.max(rtop[:, :], rprob[:, :])
                done()
                V.tensor_tensor(rdiff[:, :], rtop[:, 1:2], rtop[:, 0:1], ALU.subtract).then_inc(rdiff_ready, 1)
                V.max_index(rtop_i[:, :], rtop[:, :], rprob[:, :])
                done()
                V.tensor_copy(rtop_f[:, :], rtop_i[:, :])
                yield 46
                dve.wait_ge(params_landed, 16)
                dve.wait_ge(rw_ready, n)
                V.tensor_scalar(rw[:, 1:2], rw[:, 0:1], 1.0, None, ALU.add)
                done()
                V.reciprocal(rw[:, 2:3], rw[:, 1:2])
                done()
                V.tensor_tensor(rw[:, 3:4], rw[:, 0:1], rw[:, 2:3], ALU.mult)
                V.tensor_scalar(gate[0][:, :], par("iota_expert"), rtop_f[:, 0:1], rw[:, 2:3], ALU.is_equal, ALU.mult)
                done()
                V.tensor_scalar(gate[1][:, :], par("iota_expert"), rtop_f[:, 1:2], rw[:, 3:4], ALU.is_equal, ALU.mult)
                done()
                V.tensor_tensor(gate[0][:, :], gate[0][:, :], gate[1][:, :], ALU.add)
                yield 47
                dve.wait_ge(params_landed, 16)
                dve.wait_ge(e3_ready, n)
                done()
                V.tensor_tensor(gated[:, :, :], bank[5][:, 0:EXPERTS * D].rearrange("p (e d) -> p e d", e=EXPERTS),
                                gate[0][:, :].unsqueeze(2).to_broadcast([T, EXPERTS, D]), ALU.mult)
                done()
                V.tensor_reduce(moe[:, :], gated[:, :, :].rearrange("p e d -> p d e"), AX.X, ALU.add)
                count = value(dve, turn * 16)
                dve.wait_ge(params_landed, 16)
                dve.wait_ge(out_landed[k], count)
                done()
                V.tensor_tensor(h4[k][:, :], moe[:, :], h3[:, :], ALU.add).then_inc(h4_ready, 1)

            each_sequence(dve, before, sums, after)


def pack_params(i):
    layout, cols = param_layout()
    p = np.zeros((128, cols), np.float32)

    def put(name, a, row=0, col=0):
        a = np.asarray(a)
        if a.ndim == 1:
            a = a.reshape(-1, 1)
        at, c, r = layout[name]
        assert row + a.shape[0] <= r and col + a.shape[1] <= c, name
        p[row:row + a.shape[0], at + col:at + col + a.shape[1]] = a

    def rows(a, n=T):
        a = np.asarray(a).reshape(1, -1)
        return np.broadcast_to(a, (n, a.shape[1]))

    put("ident", np.eye(T, dtype=np.float32))
    put("causal", np.triu(np.full((T, T), LOWEST, np.float32), 1))
    put("iota_cand", rows(np.arange(NCAND, dtype=np.float32)))
    put("head_offset", rows(np.repeat(np.arange(HEADS, dtype=np.float32) * KEYS * KEYS, TOP)))
    put("iota_expert", rows(np.arange(EXPERTS, dtype=np.float32)))
    put("ones_row", np.ones((1, T), np.float32))
    put("w_ig", i["L0_tok_w_item"])
    put("w_ig", i["L0_tok_w_geo"], 64, 64)
    put("b_ig", i["L0_tok_b_item"])
    put("b_ig", i["L0_tok_b_geo"], 64)
    put("w_visit", i["L0_tok_w_visit"])
    put("b_visit", i["L0_tok_b_visit"])
    put("w_fuse_ig", i["L0_tok_w_fuse"][0:128])
    put("w_fuse_v", i["L0_tok_w_fuse"][128:192])
    put("w_fuse_v", i["L0_tok_b_fuse"].reshape(1, -1), 64)
    put("gamma", rows(i["L0_tok_ln_gamma"]))
    put("beta", rows(i["L0_tok_ln_beta"]))
    put("ln_w", i["L0_attn_ln_w"])
    put("ln_b", i["L0_attn_ln_b"])
    put("w_in", i["L0_attn_W_in"])
    put("conv_w", rows(i["L0_attn_conv_w"][:, 0, :].T, D))
    put("conv_b", i["L0_attn_conv_b"])
    put("w_xproj", i["L0_attn_W_xproj"])
    put("dt_bias", rows(i["L0_attn_dt_bias"]))
    put("a_log", rows(i["L0_attn_A_log"]))
    put("d_skip", np.repeat(i["L0_attn_Ds"], CH // SSM_HEADS))
    put("oln_w", i["L0_attn_oln_w"])
    put("oln_b", i["L0_attn_oln_b"])
    put("w_out", i["L0_attn_W_out"])
    put("wq_pk_t", i["L0_ffn_Wq_pk"].reshape(D, GROUPS, DKEY).transpose(2, 1, 0).reshape(DKEY, GROUPS * D))
    put("pk_keys_t", i["L0_ffn_pk_keys"].transpose(3, 0, 2, 1).reshape(DKEY, GROUPS * KEYS))
    put("wq", i["L0_ffn_Wq"])
    put("wo", i["L0_ffn_Wo"].reshape(HEADS // 2, 2 * D, D).transpose(1, 0, 2).reshape(2 * D, HEADS // 2 * D))
    for to, w, b in (("a_q", "Wq", "bq"), ("a_k", "Wk", "bk"), ("a_v", "Wv", "bv"), ("a_o", "Wo", "bo")):
        put(to, i["L1_attn_" + w].T)
        put(to, i["L1_attn_" + b].reshape(1, -1), D)
    for col, w, b in ((D, "Wq", "bq"), (D + 1, "Wk", "bk")):
        put("a_v", i["L1_attn_" + w][0], 0, col)
        put("a_v", i["L1_attn_" + b][0:1], D, col)
    put("r_w1", i["L1_ffn_router_w1"])
    put("r_w1", i["L1_ffn_router_b1"].reshape(1, -1), D)
    put("r_w2", i["L1_ffn_router_w2"])
    put("r_w2", i["L1_ffn_router_b2"].reshape(1, -1), ROUTER)
    for e in range(EXPERTS):
        half = (e % 2) * D
        put("e_w1", i["L1_ffn_expert_w1"][e], 0, e * D)
        put("e_w1", i["L1_ffn_expert_b1"][e:e + 1], D, e * D)
        put("e_w2", i["L1_ffn_expert_w2"][e], half, e * D)
        put("e_b2", i["L1_ffn_expert_b2"][e], half, e // 2)
        put("e_w3", i["L1_ffn_expert_w3"][e], half, e * D)
        put("e_b3", i["L1_ffn_expert_b3"][e:e + 1], 0, e * D)
    return p


def host_arrays(inputs):
    i = {k: np.asarray(v) for k, v in inputs.items()}
    return {
        "tokens": np.ascontiguousarray(i["x"]),
        "params": pack_params(i),
        "feature_table": np.concatenate([i["L0_tok_emb_table"], i["L0_tok_geo_table"], i["L0_tok_visit_table"]], axis=1),
        "memory_table": np.concatenate([i["L0_ffn_keys_table"], i["L0_ffn_values_table"]], axis=1),
    }


def kernel(**inputs):
    import concourse.bacc as _bacc
    from concourse.bass_utils import run_bass_kernel_spmd as _run

    nc = _bacc.Bacc("TRN2", target_bir_lowering=False, num_devices=1)
    arrays = host_arrays(inputs)
    args = [nc.dram_tensor(name, a.shape, mybir.dt.from_np(a.dtype), kind="ExternalInput").ap()
            for name, a in arrays.items()]
    seqs, tokens = arrays["tokens"].shape
    out = nc.dram_tensor("out", (seqs, tokens, D), F32, kind="ExternalOutput").ap()
    build_program(nc, *args, out)
    r = _run(nc, [arrays], core_ids=[0])
    return r.results[0]["out"]
```

```python
from contextlib import ExitStack

import numpy as np

import concourse.bass as bass
from concourse import mybir

ALU = mybir.AluOpType
ACT = mybir.ActivationFunctionType
AX = mybir.AxisListType
F32 = mybir.dt.float32
I32 = mybir.dt.int32
U32 = mybir.dt.uint32
BF16 = mybir.dt.bfloat16

T = 128
D = 64
ITEM, GEO, VISIT = 64, 64, 24
FEAT = ITEM + GEO + VISIT
CH = 128
SSM_HEADS, STATE = 2, 64
HEADS, KEYS, TOP = 8, 64, 16
GROUPS = 2 * HEADS
DENSE = 2
GATHERED = HEADS - DENSE
CHUNKS = KEYS * KEYS // 128
BY_TENSOR = (2, 3)
BY_VECTOR = [h for h in range(GATHERED) if h not in BY_TENSOR]
UNIT = 512 // (DENSE * T)
UNITS = CHUNKS // UNIT
RANK_PAIRS = TOP // 2
MIXER_PACE = 2.4
MIXER_START = 0.61
AFTER_START = -0.22
SELECT_PACE = 0.9
SELECT_START = 0
RANK_TICK = 12
RANK_COPY = -0.02
RANK_COMPARE = 1.25
SCALE_TICK = 14.31
HEAD_TICKS = 17.42
SCALE_PACE = 0.8
SUM_AFTER = 16.13
SUM_PACE = 1.04
DENSE_END = 90.07
AFTER_PACE = 1.88
RANK_TICKS = 2.64
UNIT_TICK = 35
PER_UNIT = 3
AFTER_WEIGHTS = 3
ROWS_AFTER = 1.0
DKEY = D // 2
PICK_HEADS = GATHERED // 2
CAND = [TOP // (i + 1) for i in range(TOP)]
NCAND = sum(CAND)
CAND_BLOCKS = [(0, 1, 16), (1, 1, 8), (2, 1, 5), (3, 1, 4), (4, 1, 3), (5, 3, 2), (8, 8, 1)]
CAND_SPACING = 65536
EXPERTS, ROUTER = 6, 32
PAIRS = EXPERTS // 2
EPS = 1e-5
LOWEST = -3.0e38
ROOT_GUESS = float(0x5F3759DF)
NEWTON_STEPS = 3
FAR_DOWN = -32768.0
LOG1P_TERMS = 8


def param_layout():
    sizes = [
        ("ident", T, T), ("causal", T, T), ("cand_base", NCAND, T), ("head_offset", GATHERED * TOP, T),
        ("iota_expert", EXPERTS, T), ("ones_row", T, 1), ("iota_key", 1, 128), ("rank_weight", RANK_PAIRS, 128),
        ("w_ig", 128, 128), ("b_ig", 1, 128), ("w_visit", D, VISIT), ("b_visit", 1, D),
        ("w_fuse_ig", D, 128), ("w_fuse_v", D, D + 1), ("gamma", D, T), ("beta", D, T),
        ("ln_w", 1, D), ("ln_b", 1, D), ("conv_b", 1, CH),
        ("w_xproj", SSM_HEADS + 2 * STATE, CH), ("dt_bias", SSM_HEADS, T), ("a_log", SSM_HEADS, T),
        ("d_skip", 1, CH), ("oln_w", 1, CH), ("oln_b", 1, CH), ("w_out", D, CH),
        ("wq", HEADS * D, D), ("wo", HEADS // 2 * D, 2 * D),
        ("a_q", D, D + 1), ("a_k", D, D + 1), ("a_v", D + 2, D + 1), ("a_o", D, D + 1),
        ("r_w1", ROUTER, D + 1), ("r_w2", EXPERTS, ROUTER + 1),
        ("e_w1", EXPERTS * D, D + 1), ("e_w2", PAIRS * 128, 128), ("e_b2", PAIRS, 128),
        ("e_w3", PAIRS * 128, 128), ("e_b3", EXPERTS * D, 1),
        ("wq_pk_t", GROUPS * D, DKEY), ("pk_keys_t", GROUPS * KEYS, DKEY), ("w_in", CH, D), ("conv_w", 3 * CH, D),
    ]
    at, out = 0, {}
    for name, cols, rows in sizes:
        out[name] = (at, cols, rows)
        at += cols
    return out, at


def build_program(nc, tokens, params, feature_table, memory_table, out):
    SEQS = tokens.shape[0]
    LAST_ITEM = feature_table.shape[0] - 1
    layout, _ = param_layout()
    ctx = ExitStack()
    with ctx:
        def sb(name, shape, dt=F32):
            return ctx.enter_context(nc.sbuf_tensor(name, shape, dt))

        def sem(name):
            return ctx.enter_context(nc.semaphore(name))

        kept = layout["wq_pk_t"][0]
        P = sb("params_sb", [128, kept])
        kv = sb("kv", [T, GATHERED, TOP, 2 * D])
        start_cols = params.shape[1] - kept
        slot_cols = TOP * 2 * D
        start_slots = -(-start_cols // slot_cols)
        start_p = kv[:, 0:start_slots, :, :].rearrange("p h k d -> p (h k d)")[:, 0:start_cols]

        def par(name):
            at, cols, r = layout[name]
            return P[0:r, at:at + cols] if at < kept else start_p[0:r, at - kept:at - kept + cols]

        w_tap = sb("w_tap", [D, 3, CH])
        neg_a = sb("neg_a", [T, SSM_HEADS])
        skip_diag = sb("skip_diag", [CH, CH])
        w_scores = sb("w_scores", [D, GROUPS * KEYS])
        tok_i = sb("tok_i", [SEQS, T], I32)
        tok_f = sb("tok_f", [SEQS, T])
        tok_ok = sb("tok_ok", [SEQS, T])
        tok_clip = sb("tok_clip", [SEQS, T])
        ids_t = sb("ids_t", [T, SEQS + 1], U32)
        ok_t = sb("ok_t", [T, SEQS])

        feat_idx = sb("feat_idx", [T, 1], U32)
        feat = [sb(f"feat{k}", [T, FEAT]) for k in range(2)]
        ig_t = sb("ig_t", [128, T])
        visit_t = sb("visit_t", [VISIT, T])
        igh_t = sb("igh_t", [128, T])
        vh_t = sb("vh_t", [D + 1, T])
        fused = sb("fused", [T, D])
        tok_mask = sb("tok_mask", [T, 1])
        stats = sb("stats", [T, 6])
        mv = sb("mv", [T, 2])
        var = sb("var", [T, 1])
        minus_half = sb("minus_half", [T, 1])
        half_bits = sb("half_bits", [T, 1], I32)
        rstd = sb("rstd", [T, 1])
        newton = sb("newton", [T, 1])
        tmp = [sb(f"tmp{k}", [T, D]) for k in range(2)]
        h0 = sb("h0", [T, D])
        src = sb("src", [T, D])
        xn = sb("xn", [T, D])
        x_t = sb("x_t", [D, T + 2])
        u_t = sb("u_t", [CH, T])
        bc_t = sb("bc_t", [STATE, 2 * T])
        z = sb("z", [T, SSM_HEADS])
        absz = sb("absz", [T, SSM_HEADS])
        ez = sb("ez", [T, SSM_HEADS])
        den = sb("den", [T, SSM_HEADS])
        s_at = sb("s_at", [T, SSM_HEADS])
        s_sq = sb("s_sq", [T, SSM_HEADS])
        poly = [sb(f"poly{k}", [T, SSM_HEADS]) for k in range(2)]
        dt_ = sb("dt", [T, SSM_HEADS])
        dt_a = sb("dt_a", [T, SSM_HEADS])
        decay = sb("decay", [T, SSM_HEADS])
        dtx = sb("dtx", [T, CH])
        l_t = sb("l_t", [T, SSM_HEADS, T])
        m_t = sb("m_t", [T, SSM_HEADS, T])
        yn = sb("yn", [T, CH])
        yn_t = sb("yn_t", [CH, T])
        h0s = sb("h0s", [T, D])
        h1_new = sb("h1_new", [T, D])
        h1 = [sb(f"h1_{k}", [T, D]) for k in range(2)]
        x2 = sb("x2", [T, D])
        x2_new = sb("x2_new", [D, T])
        x2_t = [sb(f"x2_t{k}", [D, T]) for k in range(2)]
        scores = sb("scores", [T, GROUPS, KEYS])
        scores2 = sb("scores2", [T, GROUPS, KEYS])
        top_s = sb("top_s", [T, GROUPS, TOP])
        top_i = sb("top_i", [T, GROUPS, TOP], U32)
        top_f = sb("top_f", [T, GROUPS, TOP])
        cand = sb("cand", [T, HEADS, NCAND])
        cand2 = sb("cand2", [T, HEADS, NCAND])
        cand_i = sb("cand_i", [T, GATHERED, NCAND])
        fin = sb("fin", [T, HEADS, TOP])
        fin_pos = sb("fin_pos", [T, GATHERED, TOP], U32)
        fin_posf = sb("fin_posf", [T, GATHERED, TOP])
        picked = sb("picked", [T, PICK_HEADS, TOP, NCAND])
        row_f = sb("row_f", [T, GATHERED, TOP])
        rows = [sb(f"rows{k}", [T, GATHERED, TOP], U32) for k in range(2)]
        shifted = sb("shifted", [T, HEADS, TOP])
        expo = sb("expo", [T, HEADS, TOP])
        esum = sb("esum", [T, HEADS])
        einv = [sb(f"einv{k}", [T, HEADS]) for k in range(2)]
        idx_raw = sb("idx_raw", [T, 2, DENSE, TOP])
        weight = [sb(f"weight{k}", [T, GATHERED, TOP]) for k in range(2)]

        DT = DENSE * T
        table = sb("table", [128, DENSE, CHUNKS, 2 * D])
        sel = sb("sel", [128, KEYS, KEYS], BF16)
        sel_rank = sb("sel_rank", [TOP, TOP, KEYS], BF16)
        to_key = sb("to_key", [128, 2, 128], BF16)
        cand3 = sb("cand3", [T, DENSE, NCAND])
        chosen = sb("chosen", [T, DENSE, NCAND])
        partners_n = sb("partners_n", [T, DENSE, TOP])
        sd = sb("sd", [T, DENSE, 128])
        idx_b = sb("idx_b", [TOP, 2 * DT], BF16)
        cnt_b = sb("cnt_b", [TOP, DT], BF16)
        s_hi = sb("s_hi", [128, DT], BF16)
        s_mid = sb("s_mid", [128, DT], BF16)
        s_lo = sb("s_lo", [128, DT], BF16)
        s_r1 = sb("s_r1", [128, DT])
        s_r2 = sb("s_r2", [128, DT])
        cnt_rep = [sb(f"cnt_rep{k}", [128, DT]) for k in range(2)]
        hot = [sb(f"hot{k}", [128, 2, DT], BF16) for k in range(2)]
        stair = sb("stair", [128, DT], BF16)
        short = sb("short", [128, UNIT * DT], BF16)
        push_down = sb("push_down", [128, 128], BF16)
        short_col = sb("short_col", [128, 1])
        wgt = [sb(f"wgt{k}", [128, UNIT, DENSE, T]) for k in range(2)]

        kk = sb("kk", [T, HEADS, D])
        vv = [sb(f"vv{k}", [T, HEADS, D]) for k in range(2)]
        q_t = sb("q_t", [2 * D, HEADS // 2, T])
        k_t = sb("k_t", [2 * D, HEADS // 2, T])
        sim = sb("sim", [T, HEADS, T])
        nmax = sb("nmax", [T, HEADS])
        prob = sim
        psum_row = sb("psum_row", [T, HEADS])
        prow_inv = sb("prow_inv", [T, HEADS])
        prob_t = sb("prob_t", [T, HEADS, T])
        ao = sb("ao", [T, HEADS, D])
        ao_t = sb("ao_t", [2 * D, HEADS // 2, T])
        h2 = sb("h2", [T, D])
        x3 = sb("x3", [T, D])
        x3_t = sb("x3_t", [D + 1, T])
        qk3 = sb("qk3", [D, 2 * T])
        v3 = sb("v3", [T, D + 2])
        nz3 = sb("nz3", [T, 2])
        keep3 = sb("keep3", [T, 1])
        nmax3 = sb("nmax3", [T, 1])
        nmax3s = sb("nmax3s", [T, 1])
        prob3 = sb("prob3", [T, T])
        sum3 = sb("sum3", [T, 1])
        inv3 = sb("inv3", [T, 1])
        prob3_t = sb("prob3_t", [T, T])
        o3 = sb("o3", [T, D])
        o3_t = sb("o3_t", [D + 1, T])
        h3 = sb("h3", [T, D])
        x4 = sb("x4", [T, D])
        x4_t = sb("x4_t", [D + 1, T])
        rh_t = sb("rh_t", [ROUTER + 1, T])
        rmax = sb("rmax", [T, 1])
        rexp = sb("rexp", [T, EXPERTS])
        rsum = sb("rsum", [T, 1])
        rinv = sb("rinv", [T, 1])
        rprob = sb("rprob", [T, 8])
        rtop = sb("rtop", [T, 8])
        rtop_i = sb("rtop_i", [T, 8], U32)
        rtop_f = sb("rtop_f", [T, 8])
        rdiff = sb("rdiff", [T, 1])
        rw = sb("rw", [T, 4])
        gate = [sb(f"gate{k}", [T, EXPERTS]) for k in range(2)]
        e1 = prob_t[:, 0:PAIRS, :].rearrange("p a t -> p (a t)")
        e2 = prob_t[:, PAIRS:2 * PAIRS, :].rearrange("p a t -> p (a t)")
        gated = sim[:, 0:PAIRS, :].rearrange("p a (b d) -> p (a b) d", b=2)
        moe = sb("moe", [T, D])
        h4 = [sb(f"h4_{k}", [T, D]) for k in range(2)]

        bank = [ctx.enter_context(nc.psum_tensor(f"bank{k}", [128, 512], F32)) for k in range(8)]
        A, B = bank[0:2]
        ps_scores = [B, A]
        ps_s, ps_d, ps_acc = bank[2], bank[3], bank[7]
        ps_sim = [bank[5], bank[4]]

        params_landed = sem("params_landed")
        start_params_landed = sem("start_params_landed")
        tokens_landed = sem("tokens_landed")
        consts_done = sem("consts_done")
        taps_done = sem("taps_done")
        tokens_ready = sem("tokens_ready")
        tokens_turned = sem("tokens_turned")
        ids_done = sem("ids_done")
        a_ready = sem("a_ready")
        keyprod_ready = sem("keyprod_ready")
        keyprod_taken = sem("keyprod_taken")
        feat_idx_ready = sem("feat_idx_ready")
        featT_ready = sem("featT_ready")
        featT_taken = sem("featT_taken")
        hid_ready = sem("hid_ready")
        hid_taken = sem("hid_taken")
        fused_ready = sem("fused_ready")
        fused_taken = sem("fused_taken")
        xn_ready = sem("xn_ready")
        xT_ready = sem("xT_ready")
        xT_taken = sem("xT_taken")
        uc_ready = sem("uc_ready")
        uT_ready = sem("uT_ready")
        dbc_ready = sem("dbc_ready")
        bc_taken = sem("bc_taken")
        abs_ready = sem("abs_ready")
        exp_ready = sem("exp_ready")
        dta_ready = sem("dta_ready")
        decay_ready = sem("decay_ready")
        dtx_ready = sem("dtx_ready")
        drep_ready = sem("drep_ready")
        mt_ready = sem("mt_ready")
        y_ready = sem("y_ready")
        yn_ready = sem("yn_ready")
        ynT_ready = sem("ynT_ready")
        ynT_taken = sem("ynT_taken")
        mix_ready = sem("mix_ready")
        x2_ready = sem("x2_ready")
        x2T_ready = sem("x2T_ready")
        x2T_taken = sem("x2T_taken")
        scores_ready = sem("scores_ready")
        scores_taken = sem("scores_taken")
        rows_ready = sem("rows_ready")
        shift_ready = sem("shift_ready")
        expo_ready = sem("expo_ready")
        kv_used = [sem(f"kv_used{h}") for h in range(GATHERED)]
        table_landed = sem("table_landed")
        selectors_ready = sem("selectors_ready")
        dense_in_ready = sem("dense_in_ready")
        denseT_ready = sem("denseT_ready")
        denseT_taken = sem("denseT_taken")
        split_ready = sem("split_ready")
        rank_ready = sem("rank_ready")
        cnt_taken = sem("cnt_taken")
        hot_ready = sem("hot_ready")
        stair_ready = sem("stair_ready")
        stair_taken = sem("stair_taken")
        unit_ready = sem("unit_ready")
        sum_ready = sem("sum_ready")
        short_ready = sem("short_ready")
        scaled_ready = sem("scaled_ready")
        wgt_ready = sem("wgt_ready")
        acc_ready = sem("acc_ready")
        kvsum_ready = sem("kvsum_ready")
        q_ready = sem("q_ready")
        q_taken = sem("q_taken")
        kT_ready = sem("kT_ready")
        kT_taken = sem("kT_taken")
        sim_ready = sem("sim_ready")
        max_ready = sem("max_ready")
        prob_ready = sem("prob_ready")
        probT_ready = sem("probT_ready")
        probT_taken_act = sem("probT_taken_act")
        probT_taken_dve = sem("probT_taken_dve")
        ao_ready = sem("ao_ready")
        ao_taken = sem("ao_taken")
        aoT_ready = sem("aoT_ready")
        aoT_taken = sem("aoT_taken")
        ffn_ready = sem("ffn_ready")
        x3_ready = sem("x3_ready")
        x3T_ready = sem("x3T_ready")
        x3T_taken = sem("x3T_taken")
        qkv3_ready = sem("qkv3_ready")
        qkv3_taken = sem("qkv3_taken")
        s3_ready = sem("s3_ready")
        max3_ready = sem("max3_ready")
        prob3_ready = sem("prob3_ready")
        p3T_ready = sem("p3T_ready")
        p3T_taken = sem("p3T_taken")
        o3_ready = sem("o3_ready")
        o3_taken = sem("o3_taken")
        o3T_ready = sem("o3T_ready")
        o3T_taken = sem("o3T_taken")
        proj_ready = sem("proj_ready")
        x4_ready = sem("x4_ready")
        x4T_ready = sem("x4T_ready")
        x4T_taken = sem("x4T_taken")
        r1_ready = sem("r1_ready")
        r1_taken = sem("r1_taken")
        logits_ready = sem("logits_ready")
        rmax_ready = sem("rmax_ready")
        rexp_ready = sem("rexp_ready")
        rdiff_ready = sem("rdiff_ready")
        rw_ready = sem("rw_ready")
        e1_ready = sem("e1_ready")
        e1_taken = sem("e1_taken")
        e2_ready = sem("e2_ready")
        e2_taken = sem("e2_taken")
        e3_ready = sem("e3_ready")
        h4_ready = sem("h4_ready")
        feat_landed = [sem(f"feat_landed{k}") for k in range(2)]
        kv_landed = [sem(f"kv_landed{h}") for h in range(GATHERED)]
        out_landed = [sem(f"out_landed{k}") for k in range(2)]


        def value(eng, v):
            return v if isinstance(v, int) else eng.compute_val(v)

        def weave(*parts):
            at = {part: next(part, None) for part in parts}
            while any(tick is not None for tick in at.values()):
                part = min((q for q in parts if at[q] is not None), key=lambda q: at[q])
                at[part] = next(part, None)

        def spread(scale, start, part):
            for tick in part:
                yield start + scale * tick

        def each_sequence(eng, mixer, select, dense, sums, after):
            def turn(n):
                return (n - 1) // 2 + 1, (n - 1) % 2

            def one_round(n, known=None):
                parts = []
                for ahead, scale, start, part in ((3, MIXER_PACE, MIXER_START, mixer), (0, AFTER_PACE, AFTER_START, after), (1, 1, 0, dense),
                                                  (1, 1, 0, sums), (2, SELECT_PACE, SELECT_START, select)):
                    if known is not None:
                        at, pair = known
                        m = at[ahead]
                        t, k = pair[ahead]
                    else:
                        m = n + ahead
                        if not 1 <= m <= SEQS:
                            continue
                        t, k = turn(m)
                    parts.append(spread(scale, start, part(m, t, k)))
                weave(*parts)

            for n in range(-2, 2):
                one_round(n)
            if SEQS > 4:
                with eng.Fori(0, SEQS // 2 - 2) as i:
                    at = [eng.snap(i * 2 + 2 + c) for c in range(5)]
                    turns = [eng.snap(i + 1 + c) for c in range(3)]
                    for first in range(2):
                        one_round(None, (at[first:], [(turns[(first + a + 1) // 2], (first + a + 1) % 2) for a in range(4)]))
            for n in range(SEQS - 2, SEQS + 1):
                one_round(n)

        block = ctx.enter_context(nc.Block())

        @block.sync
        def _(sp):
            sp.dma_start(start_p, params[:, kept:params.shape[1]]).then_inc(start_params_landed, 16)
            sp.dma_start(P[:, :], params[:, 0:kept]).then_inc(params_landed, 16)
            for k in range(2):
                sp.sem_inc(out_landed[k], 16)
            sp.dma_start(tok_i[:, :], tokens).then_inc(tokens_landed, 16)

            sp.dma_start(table[:, :, :, :], memory_table[GATHERED * KEYS * KEYS:HEADS * KEYS * KEYS, :]
                         .rearrange("(h c p) d -> p h c d", h=DENSE, p=128)).then_inc(table_landed, 16)

            def nothing(n, turn, k):
                yield 0

            def after(n, turn, k):
                yield 60
                sp.wait_ge(params_landed, 16)
                sp.wait_ge(h4_ready, n)
                sp.dma_start(out[bass.ds(n - 1, 1), :, :].rearrange("a t d -> (a t) d"), h4[k][:, :]).then_inc(out_landed[k], 16)

            each_sequence(sp, nothing, nothing, nothing, nothing, after)
            for k in range(2):
                sp.wait_ge(out_landed[k], 16 * (SEQS // 2) + 16)

        @block.gpsimd
        def _(pool):
            def gather_features(n, k):
                count = value(pool, n)
                pool.wait_ge(params_landed, 16)
                pool.wait_ge(feat_idx_ready, count)
                pool.indirect_dma_start(feat[k][:, :], None, feature_table,
                                        bass.IndirectOffsetOnAxis(feat_idx[:, 0:1], 0)).then_inc(feat_landed[k], 16)

            def gather_rows(n, k, ahead=True):
                if ahead:
                    gather_features(n + 2, k)
                pool.wait_ge(params_landed, 16)
                pool.wait_ge(rows_ready, n)
                for h in range(GATHERED):
                    if not (isinstance(n, int) and n == 1):
                        count = value(pool, n * 2 - 2)
                        pool.wait_ge(params_landed, 16)
                        pool.wait_ge(kv_used[h], count)
                    for t in range(TOP):
                        pool.indirect_dma_start(kv[:, h, t, :], None, memory_table,
                                                bass.IndirectOffsetOnAxis(rows[k][:, h, t:t + 1], 0)
                                                ).then_inc(kv_landed[h], 16)

            gather_features(1, 0)
            gather_features(2, 1)
            gather_rows(1, 0)
            gather_rows(2, 1)
            if SEQS > 4:
                with pool.Fori(0, SEQS // 2 - 2) as i:
                    n3, n4 = (pool.snap(i * 2 + c) for c in (3, 4))
                    gather_rows(n3, 0)
                    gather_rows(n4, 1)
            gather_rows(SEQS - 1, 0, ahead=False)
            gather_rows(SEQS, 1, ahead=False)

        @block.scalar
        def _(act):
            def copy(o, i):
                return nc.scalar.activation(o, i, ACT.Copy)

            act.wait_ge(params_landed, 16)
            nc.scalar.activation(neg_a[:, :], par("a_log"), ACT.Exp).then_inc(a_ready, 1)
            for s in range(2):
                act.wait_ge(keyprod_ready, s + 1)
                copy(w_scores[:, s * 512:(s + 1) * 512], [A, B][s][0:D, :]).then_inc(keyprod_taken, 1)
            act.wait_ge(consts_done, 1)

            def mixer(n, turn, k):
                yield 2
                act.wait_ge(params_landed, 16)
                act.wait_ge(featT_ready, n)
                copy(ig_t[:, :], A[:, 0:T])
                copy(visit_t[:, :], A[0:VISIT, T:2 * T]).then_inc(featT_taken, 1)
                yield 4
                act.wait_ge(params_landed, 16)
                act.wait_ge(hid_ready, n)
                nc.scalar.activation(igh_t[:, :], A[:, 256:384], ACT.Gelu, bias=par("b_ig"))
                nc.scalar.activation(vh_t[0:D, :], A[0:D, 384:512], ACT.Gelu, bias=par("b_visit")).then_inc(hid_taken, 1)
                yield 6
                act.wait_ge(params_landed, 16)
                act.wait_ge(fused_ready, n)
                nc.scalar.activation(fused[:, :], B[:, 0:D], ACT.Gelu).then_inc(fused_taken, 1)
                yield 17
                act.wait_ge(params_landed, 16)
                act.wait_ge(uc_ready, n)
                nc.scalar.activation(u_t[:, :], B[:, 192:320], ACT.Gelu, bias=par("conv_b")).then_inc(uT_ready, 1)
                yield 19
                act.wait_ge(params_landed, 16)
                act.wait_ge(dbc_ready, n)
                copy(bc_t[:, :], B[0:STATE, 0:2 * T]).then_inc(bc_taken, 1)
                yield 20
                act.wait_ge(params_landed, 16)
                act.wait_ge(abs_ready, n)
                nc.scalar.activation(ez[:, :], absz[:, :], ACT.Exp, scale=-1.0).then_inc(exp_ready, 1)
                yield 22
                act.wait_ge(params_landed, 16)
                act.wait_ge(dta_ready, n)
                nc.scalar.activation(decay[:, :], dt_a[:, :], ACT.Exp, scale=-1.0).then_inc(decay_ready, 1)
                for h in range(SSM_HEADS):
                    ins = nc.scalar.activation(dtx[:, h * D:(h + 1) * D], B[:, 384 + h * D:384 + (h + 1) * D],
                                               ACT.Copy, scale=dt_[:, h:h + 1])
                ins.then_inc(dtx_ready, 1)

            def select(n, turn, k):
                yield 3.5
                act.wait_ge(params_landed, 16)
                act.wait_ge(scores_ready, n)
                copy(x2_t[k][:, :], x2_new[:, :])
                if not (isinstance(n, int) and n == 1):
                    count = value(act, n - 1)
                    act.wait_ge(params_landed, 16)
                    act.wait_ge(dense_in_ready, count)
                for s in range(2):
                    ins = copy(scores[:, s * HEADS:(s + 1) * HEADS, :].rearrange("p g k -> p (g k)"), ps_scores[s][:, :])
                ins.then_inc(scores_taken, 1)
                yield 47
                act.wait_ge(params_landed, 16)
                act.wait_ge(shift_ready, n)
                nc.scalar.activation(expo[:, :, :], shifted[:, :, :], ACT.Exp).then_inc(expo_ready, 1)

            def after(n, turn, k):
                yield 1.5
                act.wait_ge(params_landed, 16)
                act.wait_ge(q_ready, n)
                copy(q_t[:, :, :].rearrange("p a t -> p (a t)"), bank[4][:, :]).then_inc(q_taken, 1)
                yield 2
                act.wait_ge(params_landed, 16)
                act.wait_ge(kT_ready, n)
                copy(k_t[:, :, :].rearrange("p a t -> p (a t)"), bank[6][:, :]).then_inc(kT_taken, 1)
                yield 7
                act.wait_ge(params_landed, 16)
                act.wait_ge(max_ready, n)
                for h in range(HEADS):
                    ins = nc.scalar.activation(prob[:, h, :], sim[:, h, :], ACT.Exp, bias=nmax[:, h:h + 1],
                                               accum_out=psum_row[:, h:h + 1])
                ins.then_inc(prob_ready, 1)
                yield 11
                act.wait_ge(params_landed, 16)
                act.wait_ge(probT_ready, n)
                copy(prob_t[:, 0:4, :].rearrange("p a t -> p (a t)"), bank[6][:, :]).then_inc(probT_taken_act, 1)
                yield 15
                act.wait_ge(params_landed, 16)
                act.wait_ge(aoT_ready, n)
                copy(ao_t[:, :, :].rearrange("p a t -> p (a t)"), bank[5][:, :]).then_inc(aoT_taken, 1)
                yield 21
                act.wait_ge(params_landed, 16)
                act.wait_ge(x3T_ready, n)
                copy(x3_t[0:D, :], bank[4][0:D, 0:T]).then_inc(x3T_taken, 1)
                yield 23
                act.wait_ge(params_landed, 16)
                act.wait_ge(qkv3_ready, n)
                copy(qk3[:, :], bank[4][0:D, T:3 * T])
                copy(v3[:, :], bank[4][:, 3 * T:3 * T + D + 2]).then_inc(qkv3_taken, 1)
                yield 26
                act.wait_ge(params_landed, 16)
                act.wait_ge(max3_ready, n)
                nc.scalar.activation(prob3[:, :], bank[5][:, 0:T], ACT.Exp, bias=nmax3s[:, :], scale=D ** -0.5,
                                     accum_out=sum3[:, :]).then_inc(prob3_ready, 1)
                yield 28
                act.wait_ge(params_landed, 16)
                act.wait_ge(p3T_ready, n)
                copy(prob3_t[:, :], bank[5][:, T:2 * T]).then_inc(p3T_taken, 1)
                yield 32
                act.wait_ge(params_landed, 16)
                act.wait_ge(o3T_ready, n)
                copy(o3_t[0:D, :], bank[5][0:D, 320:320 + T]).then_inc(o3T_taken, 1)
                yield 38
                act.wait_ge(params_landed, 16)
                act.wait_ge(x4T_ready, n)
                copy(x4_t[0:D, :], bank[6][0:D, 0:T]).then_inc(x4T_taken, 1)
                yield 40
                act.wait_ge(params_landed, 16)
                act.wait_ge(r1_ready, n)
                nc.scalar.activation(rh_t[0:ROUTER, :], bank[6][0:ROUTER, T:2 * T], ACT.Relu).then_inc(r1_taken, 1)
                yield 40
                act.wait_ge(params_landed, 16)
                act.wait_ge(e1_ready, n)
                nc.scalar.activation(e1[:, :], bank[5][:, 0:PAIRS * T], ACT.Relu).then_inc(e1_taken, 1)
                yield 43
                act.wait_ge(params_landed, 16)
                act.wait_ge(rmax_ready, n)
                nc.scalar.activation(rexp[:, :], bank[6][:, 256:256 + EXPERTS], ACT.Exp, bias=rmax[:, :],
                                     accum_out=rsum[:, :]).then_inc(rexp_ready, 1)
                yield 43.5
                act.wait_ge(params_landed, 16)
                act.wait_ge(e2_ready, n)
                for j in range(PAIRS):
                    ins = nc.scalar.activation(e2[:, j * T:(j + 1) * T], bank[4][:, j * T:(j + 1) * T], ACT.Relu,
                                               bias=par("e_b2")[:, j:j + 1])
                ins.then_inc(e2_taken, 1)
                yield 45
                act.wait_ge(params_landed, 16)
                act.wait_ge(rdiff_ready, n)
                nc.scalar.activation(rw[:, 0:1], rdiff[:, :], ACT.Exp).then_inc(rw_ready, 1)

            def dense(n, turn, k):
                yield 4
                act.wait_ge(params_landed, 16)
                act.wait_ge(denseT_ready, n)
                copy(idx_b[:, :], ps_s[0:TOP, 0:2 * DT])
                copy(cnt_b[:, :], ps_d[0:TOP, 0:DT])
                copy(s_hi[:, :], ps_d[:, 256:256 + DT]).then_inc(denseT_taken, 1)
                for c in range(RANK_PAIRS):
                    yield RANK_TICK + RANK_COPY + RANK_TICKS * c
                    count = value(act, (n - 1) * RANK_PAIRS + c + 1)
                    act.wait_ge(params_landed, 16)
                    act.wait_ge(rank_ready, count)
                    copy(cnt_rep[c % 2][:, :], ps_d[:, 0:DT]).then_inc(cnt_taken, 1)
                yield UNIT_TICK - 1
                act.wait_ge(params_landed, 16)
                act.wait_ge(stair_ready, n)
                copy(stair[:, :], ps_acc[:, 0:DT]).then_inc(stair_taken, 1)
                def fall_short(u):
                    return nc.scalar.activation(short[:, :], ps_d[:, :], ACT.Relu, bias=short_col[:, :], scale=-1.0)

                yield UNIT_TICK + 0.3
                count = value(act, (n - 1) * UNITS + 1)
                act.wait_ge(params_landed, 16)
                act.wait_ge(sum_ready, count)
                fall_short(0).then_inc(short_ready, 1)
                for u in range(UNITS):
                    yield UNIT_TICK + 1 + PER_UNIT * u
                    count = value(act, (n - 1) * UNITS + u + 1)
                    act.wait_ge(params_landed, 16)
                    act.wait_ge(unit_ready, count)
                    nc.scalar.activation(wgt[u % 2][:, :, :, :].rearrange("p c h t -> p (c h t)"), ps_s[:, :], ACT.Exp).then_inc(wgt_ready, 1)
                    if u < UNITS - 1:
                        count = value(act, (n - 1) * UNITS + u + 2)
                        act.wait_ge(params_landed, 16)
                        act.wait_ge(sum_ready, count)
                        fall_short(u + 1).then_inc(short_ready, 1)

            def sums(n, turn, k):
                for h in range(GATHERED):
                    yield SCALE_TICK + HEAD_TICKS * h
                    if h == 0:
                        act.wait_ge(params_landed, 16)
                        act.wait_ge(dense_in_ready, n)
                    count = value(act, n * TOP * 16)
                    act.wait_ge(params_landed, 16)
                    act.wait_ge(kv_landed[h], count)
                    for t in range(TOP):
                        if t % 4 == 0:
                            yield SCALE_TICK + HEAD_TICKS * h + SCALE_PACE * t
                        ins = nc.scalar.activation(kv[:, h, t, :], kv[:, h, t, :], ACT.Copy, scale=weight[k][:, h, t:t + 1])
                    ins.then_inc(scaled_ready, 1)

            def nothing(n, turn, k):
                yield 0

            each_sequence(act, mixer, select, dense, sums, after)

        @block.tensor
        def _(pe):
            mm = nc.tensor.matmul
            ident = par("ident")

            pe.wait_ge(params_landed, 16)
            pe.wait_ge(start_params_landed, 16)
            for s in range(2):
                for h in range(HEADS):
                    g = s * HEADS + h
                    ins = mm([A, B][s][0:D, h * KEYS:(h + 1) * KEYS], par("wq_pk_t")[:, g * D:(g + 1) * D],
                             par("pk_keys_t")[:, g * KEYS:(g + 1) * KEYS], start=True, stop=True)
                ins.then_inc(keyprod_ready, 1)
            pe.wait_ge(tokens_ready, 1)
            nc.tensor.transpose(ps_s[0:T, 0:SEQS], tok_clip[:, :], ident[0:SEQS, 0:SEQS])
            nc.tensor.transpose(ps_s[0:T, 128:128 + SEQS], tok_ok[:, :], ident[0:SEQS, 0:SEQS]).then_inc(tokens_turned, 1)
            pe.wait_ge(keyprod_taken, 2)
            pe.wait_ge(ids_done, 1)
            pe.wait_ge(taps_done, 1)
            pe.wait_ge(selectors_ready, 1)
            pe.wait_ge(table_landed, 16)
            pe.wait_ge(consts_done, 1)

            def mixer(n, turn, k):
                yield 1
                if not (isinstance(n, int) and n == 1):
                    count = value(pe, n - 1)
                    pe.wait_ge(params_landed, 16)
                    pe.wait_ge(scores_taken, count)
                count = value(pe, turn * 16)
                pe.wait_ge(params_landed, 16)
                pe.wait_ge(feat_landed[k], count)
                nc.tensor.transpose(A[:, 0:T], feat[k][:, 0:ITEM + GEO], ident)
                nc.tensor.transpose(A[0:VISIT, T:2 * T], feat[k][:, ITEM + GEO:FEAT], ident).then_inc(featT_ready, 1)
                yield 3
                pe.wait_ge(params_landed, 16)
                pe.wait_ge(featT_taken, n)
                mm(A[:, 256:384], par("w_ig"), ig_t[:, :], start=True, stop=True)
                mm(A[0:D, 384:512], par("w_visit"), visit_t[:, :], start=True, stop=True).then_inc(hid_ready, 1)
                yield 5
                pe.wait_ge(params_landed, 16)
                pe.wait_ge(hid_taken, n)
                mm(B[:, 0:D], igh_t[:, :], par("w_fuse_ig"), start=True, stop=False)
                mm(B[:, 0:D], vh_t[:, :], par("w_fuse_v"), start=False, stop=True).then_inc(fused_ready, 1)
                yield 14
                pe.wait_ge(params_landed, 16)
                pe.wait_ge(xn_ready, n)
                nc.tensor.transpose(B[0:D, 64:64 + T], xn[:, :], ident).then_inc(xT_ready, 1)
                yield 16
                pe.wait_ge(params_landed, 16)
                pe.wait_ge(xT_taken, n)
                for j in range(3):
                    ins = mm(B[:, 192:320], w_tap[:, j, :], x_t[:, j:j + T], start=(j == 0), stop=(j == 2))
                ins.then_inc(uc_ready, 1)
                yield 18
                pe.wait_ge(params_landed, 16)
                pe.wait_ge(uT_ready, n)
                mm(A[:, 0:SSM_HEADS], u_t[:, :], par("w_xproj")[:, 0:SSM_HEADS], start=True, stop=True)
                for j in range(2):
                    mm(B[0:STATE, j * T:(j + 1) * T], par("w_xproj")[:, SSM_HEADS + j * STATE:SSM_HEADS + (j + 1) * STATE],
                       u_t[:, :], start=True, stop=True)
                nc.tensor.transpose(B[:, 384:512], u_t[:, :], ident).then_inc(dbc_ready, 1)
                yield 23
                pe.wait_ge(params_landed, 16)
                pe.wait_ge(decay_ready, n)
                pe.wait_ge(bc_taken, n)
                mm(A[:, 256:384], bc_t[:, 0:T], bc_t[:, T:2 * T], start=True, stop=True)
                for h in range(SSM_HEADS):
                    ins = mm(A[:, h * T:(h + 1) * T], decay[:, h:h + 1].to_broadcast([T, T]), ident, start=True, stop=True)
                ins.then_inc(drep_ready, 1)
                yield 25
                pe.wait_ge(params_landed, 16)
                pe.wait_ge(mt_ready, n)
                pe.wait_ge(dtx_ready, n)
                for h in range(SSM_HEADS):
                    c = slice(h * D, (h + 1) * D)
                    o = A[:, 384 + h * D:384 + (h + 1) * D]
                    mm(o, u_t[:, :], skip_diag[:, c], start=True, stop=False)
                    ins = mm(o, m_t[:, h, :], dtx[:, c], start=False, stop=True)
                ins.then_inc(y_ready, 1)
                yield 29
                pe.wait_ge(params_landed, 16)
                pe.wait_ge(yn_ready, n)
                nc.tensor.transpose(A[:, 0:T], yn[:, :], ident).then_inc(ynT_ready, 1)
                yield 31
                pe.wait_ge(params_landed, 16)
                pe.wait_ge(ynT_taken, n)
                mm(A[:, 128:128 + D], yn_t[:, :], par("w_out"), start=True, stop=True).then_inc(mix_ready, 1)
                yield 35
                pe.wait_ge(params_landed, 16)
                pe.wait_ge(x2_ready, n)
                nc.tensor.transpose(A[0:D, 192:192 + T], x2[:, :], ident).then_inc(x2T_ready, 1)
                yield 37
                pe.wait_ge(params_landed, 16)
                pe.wait_ge(x2T_taken, n)
                for s in range(2):
                    ins = mm(ps_scores[s][:, :], x2_new[:, :], w_scores[:, s * 512:(s + 1) * 512], start=True, stop=True)
                ins.then_inc(scores_ready, 1)

            def after(n, turn, k):
                yield 1
                count = value(pe, n)
                pe.wait_ge(params_landed, 16)
                pe.wait_ge(scores_taken, count)
                for a in range(HEADS // 2):
                    ins = mm(bank[4][:, a * T:(a + 1) * T], par("wq")[:, a * 128:(a + 1) * 128], x2_t[k][:, :],
                             start=True, stop=True)
                ins.then_inc(q_ready, 1)
                yield 1
                pe.wait_ge(params_landed, 16)
                pe.wait_ge(kvsum_ready, n)
                for a in range(HEADS // 2):
                    ins = nc.tensor.transpose(bank[6][:, a * T:(a + 1) * T],
                                              kk[:, 2 * a:2 * a + 2, :].rearrange("p h d -> p (h d)"), ident)
                ins.then_inc(kT_ready, 1)
                yield 3
                pe.wait_ge(params_landed, 16)
                pe.wait_ge(q_taken, n)
                pe.wait_ge(kT_taken, n)
                for h in range(HEADS):
                    r = (h % 2) * D
                    ins = mm(ps_sim[h % 2][:, (h // 2) * T:(h // 2 + 1) * T], q_t[r:r + D, h // 2, :],
                             k_t[r:r + D, h // 2, :], start=True, stop=True)
                ins.then_inc(sim_ready, 1)
                yield 10
                pe.wait_ge(params_landed, 16)
                pe.wait_ge(prob_ready, n)
                for h in range(HEADS):
                    ins = nc.tensor.transpose(bank[6 - h // 4][:, (h % 4) * T:(h % 4 + 1) * T], prob[:, h, :], ident)
                ins.then_inc(probT_ready, 1)
                yield 12
                pe.wait_ge(params_landed, 16)
                pe.wait_ge(probT_taken_act, n)
                pe.wait_ge(probT_taken_dve, n)
                for h in range(HEADS):
                    ins = mm(bank[4][:, h * D:(h + 1) * D], prob_t[:, h, :], vv[k][:, h, :], start=True, stop=True)
                ins.then_inc(ao_ready, 1)
                yield 14
                pe.wait_ge(params_landed, 16)
                pe.wait_ge(ao_taken, n)
                for a in range(HEADS // 2):
                    ins = nc.tensor.transpose(bank[5][:, a * T:(a + 1) * T],
                                              ao[:, 2 * a:2 * a + 2, :].rearrange("p h d -> p (h d)"), ident)
                ins.then_inc(aoT_ready, 1)
                yield 16
                pe.wait_ge(params_landed, 16)
                pe.wait_ge(aoT_taken, n)
                for a in range(HEADS // 2):
                    ins = mm(bank[6][:, 0:D], ao_t[:, a, :], par("wo")[:, a * D:(a + 1) * D],
                             start=(a == 0), stop=(a == HEADS // 2 - 1))
                ins.then_inc(ffn_ready, 1)
                yield 20
                pe.wait_ge(params_landed, 16)
                pe.wait_ge(x3_ready, n)
                nc.tensor.transpose(bank[4][0:D, 0:T], x3[:, :], ident).then_inc(x3T_ready, 1)
                yield 22
                pe.wait_ge(params_landed, 16)
                pe.wait_ge(x3T_taken, n)
                mm(bank[4][0:D, T:2 * T], par("a_q"), x3_t[:, :], start=True, stop=True)
                mm(bank[4][0:D, 2 * T:3 * T], par("a_k"), x3_t[:, :], start=True, stop=True)
                mm(bank[4][:, 3 * T:3 * T + D + 2], x3_t[:, :], par("a_v"), start=True, stop=True).then_inc(qkv3_ready, 1)
                yield 24
                pe.wait_ge(params_landed, 16)
                pe.wait_ge(qkv3_taken, n)
                mm(bank[5][:, 0:T], qk3[:, 0:T], qk3[:, T:2 * T], start=True, stop=True).then_inc(s3_ready, 1)
                yield 27
                pe.wait_ge(params_landed, 16)
                pe.wait_ge(prob3_ready, n)
                nc.tensor.transpose(bank[5][:, T:2 * T], prob3[:, :], ident).then_inc(p3T_ready, 1)
                yield 29
                pe.wait_ge(params_landed, 16)
                pe.wait_ge(p3T_taken, n)
                mm(bank[5][:, 256:256 + D], prob3_t[:, :], v3[:, 0:D], start=True, stop=True).then_inc(o3_ready, 1)
                yield 31
                pe.wait_ge(params_landed, 16)
                pe.wait_ge(o3_taken, n)
                nc.tensor.transpose(bank[5][0:D, 320:320 + T], o3[:, :], ident).then_inc(o3T_ready, 1)
                yield 33
                pe.wait_ge(params_landed, 16)
                pe.wait_ge(o3T_taken, n)
                mm(bank[5][:, 448:448 + D], o3_t[:, :], par("a_o"), start=True, stop=True).then_inc(proj_ready, 1)
                yield 37
                pe.wait_ge(params_landed, 16)
                pe.wait_ge(x4_ready, n)
                nc.tensor.transpose(bank[6][0:D, 0:T], x4[:, :], ident).then_inc(x4T_ready, 1)
                yield 39
                pe.wait_ge(params_landed, 16)
                pe.wait_ge(x4T_taken, n)
                mm(bank[6][0:ROUTER, T:2 * T], par("r_w1"), x4_t[:, :], start=True, stop=True).then_inc(r1_ready, 1)
                for j in range(PAIRS):
                    ins = mm(bank[5][:, j * T:(j + 1) * T], par("e_w1")[:, j * 128:(j + 1) * 128], x4_t[:, :],
                             start=True, stop=True)
                ins.then_inc(e1_ready, 1)
                yield 41
                pe.wait_ge(params_landed, 16)
                pe.wait_ge(r1_taken, n)
                mm(bank[6][:, 256:256 + EXPERTS], rh_t[:, :], par("r_w2"), start=True, stop=True).then_inc(logits_ready, 1)
                yield 41
                pe.wait_ge(params_landed, 16)
                pe.wait_ge(e1_taken, n)
                for j in range(PAIRS):
                    ins = mm(bank[4][:, j * T:(j + 1) * T], par("e_w2")[:, j * 128:(j + 1) * 128],
                             e1[:, j * T:(j + 1) * T], start=True, stop=True)
                ins.then_inc(e2_ready, 1)
                yield 44
                pe.wait_ge(params_landed, 16)
                pe.wait_ge(e2_taken, n)
                for j in range(PAIRS):
                    c = slice(j * 128, (j + 1) * 128)
                    mm(bank[5][:, c], e2[:, j * T:(j + 1) * T], par("e_w3")[:, c], start=True, stop=False)
                    ins = mm(bank[5][:, c], par("ones_row"), par("e_b3")[:, c], start=False, stop=True)
                ins.then_inc(e3_ready, 1)

            def dense(n, turn, k):
                yield 3
                pe.wait_ge(params_landed, 16)
                pe.wait_ge(dense_in_ready, n)
                for side in range(2):
                    for h in range(DENSE):
                        q = side * DENSE + h
                        nc.tensor.transpose(ps_s[0:TOP, q * T:(q + 1) * T], idx_raw[:, side, h, :], ident)
                for h in range(DENSE):
                    nc.tensor.transpose(ps_d[0:TOP, h * T:(h + 1) * T], partners_n[:, h, :], ident)
                for h in range(DENSE):
                    ins = nc.tensor.transpose(ps_d[:, 256 + h * T:256 + (h + 1) * T], sd[:, h, :], ident)
                ins.then_inc(denseT_ready, 1)
                for c in range(RANK_PAIRS + 1):
                    if c < RANK_PAIRS:
                        yield RANK_TICK + RANK_TICKS * c
                        pe.wait_ge(params_landed, 16)
                        if c == 0:
                            pe.wait_ge(split_ready, n)
                        else:
                            count = value(pe, (n - 1) * RANK_PAIRS + c)
                            pe.wait_ge(params_landed, 16)
                            pe.wait_ge(hot_ready, count)
                        pick = sel_rank[:, 2 * c:2 * c + 2, :].rearrange("r a k -> r (a k)")
                        mm(ps_s[:, 0:2 * DT], pick, idx_b[:, :], start=True, stop=True)
                        mm(ps_d[:, 0:DT], pick, cnt_b[:, :], start=True, stop=True).then_inc(rank_ready, 1)
                    else:
                        yield RANK_TICK + RANK_TICKS * RANK_PAIRS
                        count = value(pe, n * RANK_PAIRS)
                        pe.wait_ge(params_landed, 16)
                        pe.wait_ge(hot_ready, count)
                    if c > 0:
                        for side in range(2):
                            ins = mm(ps_acc[:, 0:DT], to_key[:, side, :], hot[(c - 1) % 2][:, side, :],
                                     start=(c == 1 and side == 0), stop=(c == RANK_PAIRS and side == 1))
                ins.then_inc(stair_ready, 1)
                def chosen_sum(u):
                    for j in range(UNIT):
                        c = u * UNIT + j
                        pick = sel[:, 2 * c:2 * c + 2, :].rearrange("r a k -> r (a k)")
                        ins = mm(ps_d[:, j * DT:(j + 1) * DT], pick, stair[:, :], start=True, stop=True)
                    ins.then_inc(sum_ready, 1)

                def score_sum(u):
                    for j in range(UNIT):
                        c = u * UNIT + j
                        pick = sel[:, 2 * c:2 * c + 2, :].rearrange("r a k -> r (a k)")
                        for m, part in enumerate((s_hi, s_mid, s_lo)):
                            mm(ps_s[:, j * DT:(j + 1) * DT], pick, part[:, :], start=(j == 0 and m == 0), stop=False)

                def push_unchosen(u):
                    mm(ps_s[:, :], push_down[:, :], short[:, :], start=False, stop=True).then_inc(unit_ready, 1)

                yield UNIT_TICK
                pe.wait_ge(params_landed, 16)
                pe.wait_ge(stair_taken, n)
                chosen_sum(0)
                score_sum(0)
                yield UNIT_TICK + 0.6
                count = value(pe, (n - 1) * UNITS + 1)
                pe.wait_ge(params_landed, 16)
                pe.wait_ge(short_ready, count)
                push_unchosen(0)
                chosen_sum(1)
                for u in range(UNITS):
                    yield UNIT_TICK + AFTER_WEIGHTS + PER_UNIT * u
                    count = value(pe, (n - 1) * UNITS + u + 1)
                    pe.wait_ge(params_landed, 16)
                    pe.wait_ge(wgt_ready, count)
                    if u < UNITS - 1:
                        score_sum(u + 1)
                        count = value(pe, (n - 1) * UNITS + u + 2)
                        pe.wait_ge(params_landed, 16)
                        pe.wait_ge(short_ready, count)
                        push_unchosen(u + 1)
                    if u < UNITS - 2:
                        chosen_sum(u + 2)
                    yield UNIT_TICK + AFTER_WEIGHTS + PER_UNIT * u + ROWS_AFTER
                    for j in range(UNIT):
                        c = u * UNIT + j
                        for h in range(DENSE):
                            ins = mm(ps_acc[:, h * T:(h + 1) * T], wgt[u % 2][:, j, h, :], table[:, h, c, :],
                                     start=(c == 0 and h == 0), stop=(c == CHUNKS - 1), skip_group_check=True)
                ins.then_inc(acc_ready, 1)

            def sums(n, turn, k):
                for j, h in enumerate(BY_TENSOR):
                    yield SCALE_TICK + HEAD_TICKS * h + SUM_AFTER
                    count = value(pe, (n - 1) * GATHERED + h + 1)
                    pe.wait_ge(params_landed, 16)
                    pe.wait_ge(scaled_ready, count)
                    for t in range(TOP):
                        if t % 4 == 0 and t > 0:
                            yield SCALE_TICK + HEAD_TICKS * h + SUM_AFTER + SUM_PACE * t
                        ins = mm(ps_acc[:, DT + j * T:DT + (j + 1) * T], ident, kv[:, h, t, :], start=False,
                                 stop=(t == TOP - 1), skip_group_check=True)
                    ins.then_inc(kv_used[h], 2)

            def nothing(n, turn, k):
                yield 0

            each_sequence(pe, mixer, nothing, dense, sums, after)

        @block.vector
        def _(dve):
            V = nc.vector

            def done():
                dve.drain()

            def normalize(o, x, signal):
                V.bn_stats(stats[:, :], x)
                done()
                V.bn_aggr(mv[:, :], stats[:, :])
                done()
                V.tensor_scalar(var[:, :], mv[:, 1:2], EPS, None, ALU.add)
                V.tensor_scalar(minus_half[:, :], mv[:, 1:2], EPS, -0.5, ALU.add, ALU.mult)
                done()
                V.tensor_scalar(half_bits[:, :], var[:, :].bitcast(I32), 1, None, ALU.logical_shift_right)
                done()
                V.tensor_scalar(rstd[:, :].bitcast(I32), half_bits[:, :], -1.0, ROOT_GUESS, ALU.mult, ALU.add)
                done()
                for _ in range(NEWTON_STEPS):
                    V.scalar_tensor_tensor(newton[:, :], rstd[:, :], minus_half[:, :], rstd[:, :], ALU.mult, ALU.mult)
                    done()
                    V.scalar_tensor_tensor(rstd[:, :], newton[:, :], 1.5, rstd[:, :], ALU.add, ALU.mult)
                    done()
                ins = V.tensor_scalar(o, x, mv[:, 0:1], rstd[:, :], ALU.subtract, ALU.mult)
                if signal is not None:
                    ins.then_inc(signal, 1)

            for x, v in ((short_col[:, :], TOP + 1.0), (x_t[:, 0:1], 0.0), (x_t[:, T + 1:T + 2], 0.0),
                         (vh_t[D:D + 1, :], 1.0), (x3_t[D:D + 1, :], 1.0), (o3_t[D:D + 1, :], 1.0),
                         (x4_t[D:D + 1, :], 1.0), (rh_t[ROUTER:ROUTER + 1, :], 1.0), (rprob[:, :], -1.0)):
                ins = V.memset(x, v)
            ins.then_inc(consts_done, 1)
            dve.wait_ge(params_landed, 16)
            dve.wait_ge(start_params_landed, 16)
            V.tensor_scalar(skip_diag[:, :], par("ident"), par("d_skip"), None, ALU.mult)
            for j in range(3):
                ins = V.tensor_tensor(w_tap[:, j, :], par("w_in"), par("conv_w")[:, j * CH:(j + 1) * CH], ALU.mult)
            ins.then_inc(taps_done, 1)
            V.memset(to_key[:, :, :], 0.0)
            V.tensor_scalar(push_down[:, :], par("ident"), FAR_DOWN, None, ALU.mult)
            V.tensor_copy(sel[0:KEYS, :, :], par("ident")[0:KEYS, 0:KEYS].unsqueeze(1).to_broadcast([KEYS, KEYS, KEYS]))
            V.tensor_copy(sel[KEYS:128, :, :], par("ident")[KEYS:128, KEYS:128].unsqueeze(2).to_broadcast([KEYS, KEYS, KEYS]))
            V.tensor_copy(sel_rank[:, :, :], par("ident")[0:TOP, 0:TOP].unsqueeze(2).to_broadcast([TOP, TOP, KEYS]))
            done()
            for side in range(2):
                for r in range(2):
                    rows_r = slice(r * KEYS, (r + 1) * KEYS)
                    ins = V.tensor_copy(to_key[rows_r, side, side * KEYS:(side + 1) * KEYS], par("ident")[rows_r, rows_r])
            ins.then_inc(selectors_ready, 1)
            dve.wait_ge(tokens_landed, 16)
            V.tensor_copy(tok_f[:, :], tok_i[:, :])
            done()
            V.tensor_scalar(tok_ok[:, :], tok_f[:, :], 0.0, 0.1, ALU.not_equal, ALU.mult)
            V.tensor_scalar(tok_clip[:, :], tok_f[:, :], 0.0, float(LAST_ITEM), ALU.max, ALU.min).then_inc(tokens_ready, 1)
            dve.wait_ge(tokens_turned, 1)
            V.tensor_copy(ids_t[:, 0:SEQS], ps_s[0:T, 0:SEQS])
            V.tensor_copy(ids_t[:, SEQS:SEQS + 1], ps_s[0:T, 0:1])
            V.tensor_copy(ok_t[:, :], ps_s[0:T, 128:128 + SEQS]).then_inc(ids_done, 1)
            done()
            V.tensor_copy(feat_idx[:, :], ids_t[:, 0:1]).then_inc(feat_idx_ready, 1)
            dve.wait_ge(a_ready, 1)

            def top16(tick, step, values, spare, tops, places, placed):
                n = values.shape[1]
                for g in range(n):
                    V.max(tops[:, g, 0:8], values[:, g, :])
                done()
                yield tick + step
                for g in range(n):
                    V.match_replace(spare[:, g, :], tops[:, g, 0:8], values[:, g, :], LOWEST)
                for g in range(placed):
                    V.max_index(places[:, g, 0:8], tops[:, g, 0:8], values[:, g, :])
                done()
                yield tick + 3 * step
                for g in range(n):
                    V.max(tops[:, g, 8:16], spare[:, g, :])
                done()
                yield tick + 4 * step
                for g in range(placed):
                    V.max_index(places[:, g, 8:16], tops[:, g, 8:16], spare[:, g, :])
                done()

            def mixer(n, turn, k):
                yield 1
                count = value(dve, turn * 16)
                dve.wait_ge(params_landed, 16)
                dve.wait_ge(feat_landed[k], count)
                V.tensor_copy(feat_idx[:, :], ids_t[:, bass.ds(n, 1)]).then_inc(feat_idx_ready, 1)
                V.tensor_copy(tok_mask[:, :], ok_t[:, bass.ds(n - 1, 1)])
                yield 7
                dve.wait_ge(params_landed, 16)
                dve.wait_ge(fused_taken, n)
                yield 9
                normalize(tmp[0][:, :], fused[:, :], None)
                done()
                V.tensor_tensor(tmp[1][:, :], tmp[0][:, :], par("gamma"), ALU.mult)
                done()
                V.tensor_tensor(tmp[0][:, :], tmp[1][:, :], par("beta"), ALU.add)
                done()
                V.scalar_tensor_tensor(h0[:, :], tmp[0][:, :], tok_mask[:, :], feat[k][:, 0:D], ALU.mult, ALU.add)
                done()
                yield 11
                normalize(src[:, :], h0[:, :], None)
                done()
                yield 13
                normalize(xn[:, :], src[:, :], xn_ready)
                V.tensor_tensor(h0s[:, :], h0[:, :], src[:, :], ALU.add)
                yield 15
                dve.wait_ge(params_landed, 16)
                dve.wait_ge(xT_ready, n)
                V.tensor_scalar(x_t[:, 1:T + 1], B[0:D, 64:64 + T], par("ln_w"), par("ln_b"), ALU.mult, ALU.add).then_inc(xT_taken, 1)
                yield 19
                dve.wait_ge(params_landed, 16)
                dve.wait_ge(dbc_ready, n)
                V.tensor_tensor(z[:, :], A[:, 0:SSM_HEADS], par("dt_bias"), ALU.add)
                done()
                V.scalar_tensor_tensor(absz[:, :], z[:, :], -1.0, z[:, :], ALU.mult, ALU.max).then_inc(abs_ready, 1)
                yield 21
                dve.wait_ge(params_landed, 16)
                dve.wait_ge(exp_ready, n)
                V.tensor_scalar(den[:, :], ez[:, :], 2.0, None, ALU.add)
                done()
                V.reciprocal(absz[:, :], den[:, :])
                done()
                V.tensor_tensor(s_at[:, :], ez[:, :], absz[:, :], ALU.mult)
                done()
                V.tensor_tensor(s_sq[:, :], s_at[:, :], s_at[:, :], ALU.mult)
                done()
                V.tensor_scalar(poly[0][:, :], s_sq[:, :], 1.0 / (2 * LOG1P_TERMS + 1), None, ALU.mult)
                at = 0
                for j in range(LOG1P_TERMS - 1, 0, -1):
                    done()
                    V.scalar_tensor_tensor(poly[1 - at][:, :], poly[at][:, :], 1.0 / (2 * j + 1), s_sq[:, :], ALU.add, ALU.mult)
                    at = 1 - at
                done()
                V.scalar_tensor_tensor(poly[1 - at][:, :], poly[at][:, :], 1.0, s_at[:, :], ALU.add, ALU.mult)
                V.tensor_scalar(den[:, :], z[:, :], 0.0, None, ALU.max)
                done()
                V.scalar_tensor_tensor(dt_[:, :], poly[1 - at][:, :], 2.0, den[:, :], ALU.mult, ALU.add)
                done()
                V.tensor_tensor(dt_a[:, :], dt_[:, :], neg_a[:, :], ALU.mult).then_inc(dta_ready, 1)
                yield 24
                dve.wait_ge(params_landed, 16)
                dve.wait_ge(drep_ready, n)
                for h in range(SSM_HEADS):
                    V.tensor_tensor_scan(l_t[:, h, :], A[:, h * T:(h + 1) * T], par("ident"), 0.0, ALU.mult, ALU.add)
                done()
                for h in range(SSM_HEADS):
                    ins = V.tensor_tensor(m_t[:, h, :], A[:, 256:384], l_t[:, h, :], ALU.mult)
                ins.then_inc(mt_ready, 1)
                yield 26
                dve.wait_ge(params_landed, 16)
                dve.wait_ge(y_ready, n)
                yield 28
                normalize(yn[:, :], A[:, 384:512], yn_ready)
                yield 30
                dve.wait_ge(params_landed, 16)
                dve.wait_ge(ynT_ready, n)
                V.tensor_scalar(yn_t[:, :], A[:, 0:T], par("oln_w"), par("oln_b"), ALU.mult, ALU.add).then_inc(ynT_taken, 1)
                yield 32
                dve.wait_ge(params_landed, 16)
                dve.wait_ge(mix_ready, n)
                V.tensor_tensor(h1_new[:, :], A[:, 128:128 + D], h0s[:, :], ALU.add)
                done()
                yield 34
                normalize(x2[:, :], h1_new[:, :], x2_ready)
                yield 36
                dve.wait_ge(params_landed, 16)
                dve.wait_ge(x2T_ready, n)
                V.tensor_copy(x2_new[:, :], A[0:D, 192:192 + T]).then_inc(x2T_taken, 1)

            def select(n, turn, k):
                yield 4
                count = value(dve, n)
                dve.wait_ge(params_landed, 16)
                dve.wait_ge(scores_taken, count)
                yield from top16(4, 5, scores, scores2, top_s, top_i, GROUPS)
                yield 28
                V.tensor_copy(top_f[:, :, :], top_i[:, :, :])
                done()
                for side in range(2):
                    V.tensor_copy(idx_raw[:, side, :, :], top_i[:, side * HEADS + GATHERED:(side + 1) * HEADS, :])
                V.scalar_tensor_tensor(top_f[:, HEADS:HEADS + GATHERED, :].rearrange("p h k -> p (h k)"),
                                       top_f[:, HEADS:HEADS + GATHERED, :].rearrange("p h k -> p (h k)"), float(KEYS),
                                       par("head_offset"), ALU.mult, ALU.add)
                done()
                at = 0
                for first, ranks, partners in CAND_BLOCKS:
                    for of, o, heads in ((top_s, cand, HEADS), (top_f, cand_i, GATHERED)):
                        shape = [T, heads, ranks, partners]
                        V.tensor_tensor(o[:, :, at:at + ranks * partners].rearrange("p h (a b) -> p h a b", a=ranks),
                                        of[:, 0:heads, first:first + ranks].unsqueeze(3).to_broadcast(shape),
                                        of[:, HEADS:HEADS + heads, 0:partners].unsqueeze(2).to_broadcast(shape), ALU.add)
                    at += ranks * partners
                done()
                V.tensor_tensor(cand_i[:, :, :], cand_i[:, :, :],
                                par("cand_base").unsqueeze(1).to_broadcast([T, GATHERED, NCAND]), ALU.add)
                yield from top16(33, 3, cand, cand2, fin, fin_pos, GATHERED)
                yield 46
                V.tensor_copy(h1[k][:, :], h1_new[:, :])
                V.tensor_scalar(fin_posf[:, :, :], fin_pos[:, :, :], float(CAND_SPACING), None, ALU.mult)
                V.tensor_tensor(shifted[:, :, :], fin[:, :, :], fin[:, :, 0:1].to_broadcast([T, HEADS, TOP]),
                                ALU.subtract).then_inc(shift_ready, 1)
                done()
                shape = [T, PICK_HEADS, TOP, NCAND]
                for half in range(GATHERED // PICK_HEADS):
                    heads = slice(half * PICK_HEADS, (half + 1) * PICK_HEADS)
                    yield 50 + 18 * half
                    V.tensor_tensor(picked[:, :, :, :], cand_i[:, heads, :].unsqueeze(2).to_broadcast(shape),
                                    fin_posf[:, heads, :].unsqueeze(3).to_broadcast(shape), ALU.subtract)
                    done()
                    yield 59 + 18 * half
                    V.tensor_reduce(row_f[:, heads, :], picked[:, :, :, :], AX.X, ALU.min, apply_absolute_value=True)
                    done()
                V.tensor_copy(rows[k][:, :, :], row_f[:, :, :]).then_inc(rows_ready, 1)
                yield 90
                dve.wait_ge(params_landed, 16)
                dve.wait_ge(expo_ready, n)
                V.tensor_reduce(esum[:, :], expo[:, :, :], AX.X, ALU.add)
                done()
                V.reciprocal(einv[k][:, :], esum[:, :])
                done()
                V.tensor_tensor(weight[k][:, :, :], expo[:, 0:GATHERED, :],
                                einv[k][:, 0:GATHERED].unsqueeze(2).to_broadcast([T, GATHERED, TOP]), ALU.mult)
                yield 94
                for h in range(DENSE):
                    g = GATHERED + h
                    V.match_replace(cand3[:, h, :], fin[:, g, 8:16], cand2[:, g, :], LOWEST)
                    for side in range(2):
                        V.tensor_scalar(sd[:, h, side * KEYS:(side + 1) * KEYS], scores[:, side * HEADS + g, :],
                                        top_s[:, side * HEADS + g, 0:1], None, ALU.subtract)
                done()
                V.tensor_scalar(chosen[:, :, :], cand3[:, :, :], 0.5 * LOWEST, None, ALU.is_lt)
                done()
                at = 0
                for first, ranks, partners in CAND_BLOCKS:
                    ins = V.tensor_reduce(partners_n[:, :, first:first + ranks],
                                          chosen[:, :, at:at + ranks * partners].rearrange("p h (a b) -> p h a b", a=ranks),
                                          AX.X, ALU.add)
                    at += ranks * partners
                ins.then_inc(dense_in_ready, 1)

            def dense(n, turn, k):
                yield 5
                dve.wait_ge(params_landed, 16)
                dve.wait_ge(denseT_taken, n)
                V.tensor_tensor(s_r1[:, :], ps_d[:, 256:256 + DT], s_hi[:, :], ALU.subtract)
                done()
                V.tensor_copy(s_mid[:, :], s_r1[:, :])
                done()
                V.tensor_tensor(s_r2[:, :], s_r1[:, :], s_mid[:, :], ALU.subtract)
                done()
                V.tensor_copy(s_lo[:, :], s_r2[:, :]).then_inc(split_ready, 1)
                for c in range(RANK_PAIRS):
                    yield RANK_TICK + RANK_COMPARE + RANK_TICKS * c
                    count = value(dve, (n - 1) * RANK_PAIRS + c + 1)
                    dve.wait_ge(params_landed, 16)
                    dve.wait_ge(cnt_taken, count)
                    V.scalar_tensor_tensor(hot[c % 2][:, 0, :], ps_s[:, 0:DT], par("iota_key"), cnt_rep[c % 2][:, :],
                                           ALU.is_equal, ALU.mult)
                    V.tensor_scalar(hot[c % 2][:, 1, :], ps_s[:, DT:2 * DT], par("iota_key"),
                                    par("rank_weight")[:, c:c + 1], ALU.is_equal, ALU.mult).then_inc(hot_ready, 1)
                yield DENSE_END
                count = value(dve, n * 2)
                dve.wait_ge(params_landed, 16)
                dve.wait_ge(acc_ready, n)
                dve.wait_ge(params_landed, 16)
                dve.wait_ge(kv_used[BY_TENSOR[-1]], count)
                by_pe = slice(BY_TENSOR[0], BY_TENSOR[-1] + 1)
                pe_sums = ps_acc[:, DT:DT + len(BY_TENSOR) * T].rearrange("p (h d) -> p h d", d=2 * D)
                V.tensor_copy(kk[:, by_pe, :], pe_sums[:, :, 0:D])
                V.tensor_copy(vv[k][:, by_pe, :], pe_sums[:, :, D:2 * D])
                for h in range(DENSE):
                    g = GATHERED + h
                    V.tensor_scalar(kk[:, g, :], ps_acc[:, h * T:h * T + D], einv[k][:, g:g + 1], None, ALU.mult)
                    V.tensor_scalar(vv[k][:, g, :], ps_acc[:, h * T + D:(h + 1) * T], einv[k][:, g:g + 1], None, ALU.mult)

            def sums(n, turn, k):
                for h in BY_VECTOR:
                    yield SCALE_TICK + HEAD_TICKS * h + SUM_AFTER
                    count = value(dve, (n - 1) * GATHERED + h + 1)
                    dve.wait_ge(params_landed, 16)
                    dve.wait_ge(scaled_ready, count)
                    V.tensor_reduce(kk[:, h, :], kv[:, h, :, 0:D].rearrange("p k d -> p d k"), AX.X, ALU.add).then_inc(kv_used[h], 1)
                    ins = V.tensor_reduce(vv[k][:, h, :], kv[:, h, :, D:2 * D].rearrange("p k d -> p d k"), AX.X, ALU.add)
                    ins.then_inc(kv_used[h], 1)
                yield 125
                done()
                dve.sem_inc(kvsum_ready, 1)

            def after(n, turn, k):
                yield 4
                dve.wait_ge(params_landed, 16)
                dve.wait_ge(sim_ready, n)
                for a in range(2):
                    V.scalar_tensor_tensor(sim[:, a:HEADS:2, :], ps_sim[a][:, :].rearrange("p (h t) -> p h t", h=4), D ** -0.5,
                                           par("causal").unsqueeze(1).to_broadcast([T, 4, T]), ALU.mult, ALU.add)
                done()
                V.tensor_reduce(nmax[:, :], sim[:, :, :], AX.X, ALU.max, negate=True).then_inc(max_ready, 1)
                yield 10.5
                dve.wait_ge(params_landed, 16)
                dve.wait_ge(prob_ready, n)
                V.reciprocal(prow_inv[:, :], psum_row[:, :])
                yield 11
                dve.wait_ge(params_landed, 16)
                dve.wait_ge(probT_ready, n)
                V.tensor_copy(prob_t[:, 4:8, :].rearrange("p a t -> p (a t)"), bank[5][:, :]).then_inc(probT_taken_dve, 1)
                yield 13
                dve.wait_ge(params_landed, 16)
                dve.wait_ge(ao_ready, n)
                V.tensor_tensor(ao[:, :, :], bank[4][:, :].rearrange("p (h d) -> p h d", h=HEADS),
                                prow_inv[:, :].unsqueeze(2).to_broadcast([T, HEADS, D]), ALU.mult).then_inc(ao_taken, 1)
                yield 17
                dve.wait_ge(params_landed, 16)
                dve.wait_ge(ffn_ready, n)
                V.tensor_tensor(h2[:, :], bank[6][:, 0:D], h1[k][:, :], ALU.add)
                done()
                yield 19
                normalize(x3[:, :], h2[:, :], x3_ready)
                yield 25
                dve.wait_ge(params_landed, 16)
                dve.wait_ge(s3_ready, n)
                V.tensor_reduce(nmax3[:, :], bank[5][:, 0:T], AX.X, ALU.max, negate=True)
                V.tensor_scalar(nz3[:, :], v3[:, D:D + 2], 0.0, None, ALU.not_equal)
                done()
                V.tensor_scalar(nmax3s[:, :], nmax3[:, :], D ** -0.5, None, ALU.mult).then_inc(max3_ready, 1)
                V.tensor_tensor(keep3[:, :], nz3[:, 0:1], nz3[:, 1:2], ALU.mult)
                yield 27
                dve.wait_ge(params_landed, 16)
                dve.wait_ge(prob3_ready, n)
                V.reciprocal(inv3[:, :], sum3[:, :])
                yield 30
                dve.wait_ge(params_landed, 16)
                dve.wait_ge(o3_ready, n)
                done()
                V.tensor_scalar(o3[:, :], bank[5][:, 256:256 + D], inv3[:, :], keep3[:, :], ALU.mult, ALU.mult).then_inc(o3_taken, 1)
                yield 34
                dve.wait_ge(params_landed, 16)
                dve.wait_ge(proj_ready, n)
                V.tensor_tensor(h3[:, :], bank[5][:, 448:448 + D], h2[:, :], ALU.add)
                done()
                yield 36
                normalize(x4[:, :], h3[:, :], x4_ready)
                yield 42
                dve.wait_ge(params_landed, 16)
                dve.wait_ge(logits_ready, n)
                V.tensor_reduce(rmax[:, :], bank[6][:, 256:256 + EXPERTS], AX.X, ALU.max, negate=True).then_inc(rmax_ready, 1)
                yield 44
                dve.wait_ge(params_landed, 16)
                dve.wait_ge(rexp_ready, n)
                V.reciprocal(rinv[:, :], rsum[:, :])
                done()
                V.tensor_scalar(rprob[:, 0:EXPERTS], rexp[:, :], rinv[:, :], None, ALU.mult)
                done()
                V.max(rtop[:, :], rprob[:, :])
                done()
                V.tensor_tensor(rdiff[:, :], rtop[:, 1:2], rtop[:, 0:1], ALU.subtract).then_inc(rdiff_ready, 1)
                V.max_index(rtop_i[:, :], rtop[:, :], rprob[:, :])
                done()
                V.tensor_copy(rtop_f[:, :], rtop_i[:, :])
                yield 46
                dve.wait_ge(params_landed, 16)
                dve.wait_ge(rw_ready, n)
                V.tensor_scalar(rw[:, 1:2], rw[:, 0:1], 1.0, None, ALU.add)
                done()
                V.reciprocal(rw[:, 2:3], rw[:, 1:2])
                done()
                V.tensor_tensor(rw[:, 3:4], rw[:, 0:1], rw[:, 2:3], ALU.mult)
                V.tensor_scalar(gate[0][:, :], par("iota_expert"), rtop_f[:, 0:1], rw[:, 2:3], ALU.is_equal, ALU.mult)
                done()
                V.tensor_scalar(gate[1][:, :], par("iota_expert"), rtop_f[:, 1:2], rw[:, 3:4], ALU.is_equal, ALU.mult)
                done()
                V.tensor_tensor(gate[0][:, :], gate[0][:, :], gate[1][:, :], ALU.add)
                yield 47
                dve.wait_ge(params_landed, 16)
                dve.wait_ge(e3_ready, n)
                done()
                V.tensor_tensor(gated[:, :, :], bank[5][:, 0:EXPERTS * D].rearrange("p (e d) -> p e d", e=EXPERTS),
                                gate[0][:, :].unsqueeze(2).to_broadcast([T, EXPERTS, D]), ALU.mult)
                done()
                V.tensor_reduce(moe[:, :], gated[:, :, :].rearrange("p e d -> p d e"), AX.X, ALU.add)
                count = value(dve, turn * 16)
                dve.wait_ge(params_landed, 16)
                dve.wait_ge(out_landed[k], count)
                done()
                V.tensor_tensor(h4[k][:, :], moe[:, :], h3[:, :], ALU.add).then_inc(h4_ready, 1)

            each_sequence(dve, mixer, select, dense, sums, after)


def pack_params(i):
    layout, cols = param_layout()
    p = np.zeros((128, cols), np.float32)

    def put(name, a, row=0, col=0):
        a = np.asarray(a)
        if a.ndim == 1:
            a = a.reshape(-1, 1)
        at, c, r = layout[name]
        assert row + a.shape[0] <= r and col + a.shape[1] <= c, name
        p[row:row + a.shape[0], at + col:at + col + a.shape[1]] = a

    def rows(a, n=T):
        a = np.asarray(a).reshape(1, -1)
        return np.broadcast_to(a, (n, a.shape[1]))

    put("ident", np.eye(T, dtype=np.float32))
    put("causal", np.triu(np.full((T, T), LOWEST, np.float32), 1))
    put("cand_base", rows(np.arange(NCAND, dtype=np.float32) * CAND_SPACING))
    put("head_offset", rows(np.repeat(np.arange(GATHERED, dtype=np.float32) * KEYS * KEYS, TOP)))
    put("iota_expert", rows(np.arange(EXPERTS, dtype=np.float32)))
    put("ones_row", np.ones((1, T), np.float32))
    put("iota_key", np.arange(128, dtype=np.float32) % KEYS)
    put("rank_weight", TOP - (2 * np.arange(RANK_PAIRS, dtype=np.float32)[None, :] + np.arange(128)[:, None] // KEYS))
    put("w_ig", i["L0_tok_w_item"])
    put("w_ig", i["L0_tok_w_geo"], 64, 64)
    put("b_ig", i["L0_tok_b_item"])
    put("b_ig", i["L0_tok_b_geo"], 64)
    put("w_visit", i["L0_tok_w_visit"])
    put("b_visit", i["L0_tok_b_visit"])
    put("w_fuse_ig", i["L0_tok_w_fuse"][0:128])
    put("w_fuse_v", i["L0_tok_w_fuse"][128:192])
    put("w_fuse_v", i["L0_tok_b_fuse"].reshape(1, -1), 64)
    put("gamma", rows(i["L0_tok_ln_gamma"]))
    put("beta", rows(i["L0_tok_ln_beta"]))
    put("ln_w", i["L0_attn_ln_w"])
    put("ln_b", i["L0_attn_ln_b"])
    put("w_in", i["L0_attn_W_in"])
    put("conv_w", rows(i["L0_attn_conv_w"][:, 0, :].T, D))
    put("conv_b", i["L0_attn_conv_b"])
    put("w_xproj", i["L0_attn_W_xproj"])
    put("dt_bias", rows(i["L0_attn_dt_bias"]))
    put("a_log", rows(i["L0_attn_A_log"]))
    put("d_skip", np.repeat(i["L0_attn_Ds"], CH // SSM_HEADS))
    put("oln_w", i["L0_attn_oln_w"])
    put("oln_b", i["L0_attn_oln_b"])
    put("w_out", i["L0_attn_W_out"])
    put("wq_pk_t", i["L0_ffn_Wq_pk"].reshape(D, GROUPS, DKEY).transpose(2, 1, 0).reshape(DKEY, GROUPS * D))
    put("pk_keys_t", i["L0_ffn_pk_keys"].transpose(3, 0, 2, 1).reshape(DKEY, GROUPS * KEYS))
    put("wq", i["L0_ffn_Wq"])
    put("wo", i["L0_ffn_Wo"].reshape(HEADS // 2, 2 * D, D).transpose(1, 0, 2).reshape(2 * D, HEADS // 2 * D))
    for to, w, b in (("a_q", "Wq", "bq"), ("a_k", "Wk", "bk"), ("a_v", "Wv", "bv"), ("a_o", "Wo", "bo")):
        put(to, i["L1_attn_" + w].T)
        put(to, i["L1_attn_" + b].reshape(1, -1), D)
    for col, w, b in ((D, "Wq", "bq"), (D + 1, "Wk", "bk")):
        put("a_v", i["L1_attn_" + w][0], 0, col)
        put("a_v", i["L1_attn_" + b][0:1], D, col)
    put("r_w1", i["L1_ffn_router_w1"])
    put("r_w1", i["L1_ffn_router_b1"].reshape(1, -1), D)
    put("r_w2", i["L1_ffn_router_w2"])
    put("r_w2", i["L1_ffn_router_b2"].reshape(1, -1), ROUTER)
    for e in range(EXPERTS):
        half = (e % 2) * D
        put("e_w1", i["L1_ffn_expert_w1"][e], 0, e * D)
        put("e_w1", i["L1_ffn_expert_b1"][e:e + 1], D, e * D)
        put("e_w2", i["L1_ffn_expert_w2"][e], half, e * D)
        put("e_b2", i["L1_ffn_expert_b2"][e], half, e // 2)
        put("e_w3", i["L1_ffn_expert_w3"][e], half, e * D)
        put("e_b3", i["L1_ffn_expert_b3"][e:e + 1], 0, e * D)
    return p


def host_arrays(inputs):
    i = {k: np.asarray(v) for k, v in inputs.items()}
    return {
        "tokens": np.ascontiguousarray(i["x"]),
        "params": pack_params(i),
        "feature_table": np.concatenate([i["L0_tok_emb_table"], i["L0_tok_geo_table"], i["L0_tok_visit_table"]], axis=1),
        "memory_table": np.concatenate([i["L0_ffn_keys_table"], i["L0_ffn_values_table"]], axis=1),
    }


def kernel(**inputs):
    import concourse.bacc as _bacc
    from concourse.bass_utils import run_bass_kernel_spmd as _run

    nc = _bacc.Bacc("TRN2", target_bir_lowering=False, num_devices=1)
    arrays = host_arrays(inputs)
    args = [nc.dram_tensor(name, a.shape, mybir.dt.from_np(a.dtype), kind="ExternalInput").ap()
            for name, a in arrays.items()]
    seqs, tokens = arrays["tokens"].shape
    out = nc.dram_tensor("out", (seqs, tokens, D), F32, kind="ExternalOutput").ap()
    build_program(nc, *args, out)
    r = _run(nc, [arrays], core_ids=[0])
    return r.results[0]["out"]
```
